# Optimizing a Trainium2 kernel written in Bass

```python
import numpy as np
import jax
import jax.numpy as jnp

def _softmax(x, axis=-1):
    return jax.nn.softmax(x, axis=axis)
def _gelu(x):
    return jax.nn.gelu(x, approximate=True)
def _silu(x):
    return jax.nn.silu(x)
def _sigmoid(x):
    return jax.nn.sigmoid(x)
def _layernorm(x, axis=-1, eps=1e-5):
    m = jnp.mean(x, axis=axis, keepdims=True)
    v = jnp.var(x, axis=axis, keepdims=True)
    return (x - m) / jnp.sqrt(v + eps)
def _scatter_add(tgt, idx, src, axis=0):
    return tgt.at[idx].add(src)
def _segment_sum(src, seg, n):
    return jax.ops.segment_sum(src, seg, n)

kernel_name = 'mk_conv_preact_d4_conv_nchw32_ce6e27'

def setup_inputs(seed: int = 0):
    np.random.seed(seed)
    _w = jnp.asarray
    def _rec_inputs():
        import jax
        import jax.numpy as jnp
        _gk = jax.random.key(seed)
        x = -0.000125 + 0.9999 * jax.random.normal(jax.random.fold_in(_gk, 1), (16, 32, 256, 256), jnp.float32)
        return x
    x = _rec_inputs()
    def _L0_conv_setup():
        import jax, jax.numpy as jnp
        import numpy as np
        B, IN_CH, OUT_CH, R = (16, 32, 32, 32)
        M1, M2 = (32, 32)
        H, W = (256, 256)
        key = jax.random.key(seed)
        k1, k2, k3, k4 = jax.random.split(key, 4)
        x = jax.random.normal(k1, (B, IN_CH, H, W), jnp.float32)
        coeff_real = jax.random.normal(k2, (R, M1, M2, IN_CH), jnp.float32)
        coeff_imag = jax.random.normal(k3, (R, M1, M2, IN_CH), jnp.float32)
        proj = jax.random.normal(k4, (OUT_CH, R), jnp.float32)
        return {'x': x, 'coeff_real': coeff_real, 'coeff_imag': coeff_imag, 'proj': proj}
    _L0_conv_all = _L0_conv_setup()
    _L0_conv_in = {k: v for k, v in _L0_conv_all.items() if k in ('coeff_real', 'coeff_imag', 'proj', )}
    del _L0_conv_all

    def _L1_conv_setup():
        import jax, jax.numpy as jnp
        import numpy as np
        B, C, H, W = (16, 32, 256, 256)

        def _dir_scan(xT, w_seq):

            def step(prev, xs):
                xr, wr = xs
                new = jnp.maximum(wr * prev + xr, 0.0)
                return (new, new)
            _, outs = jax.lax.scan(step, xT[0], (xT[1:], w_seq))
            return jnp.concatenate([xT[:1], outs], axis=0)

        def _forward(inp, weights, conv_w, conv_b):
            w_up, w_down, w_left, w_right = jax.nn.sigmoid(weights)
            xH = jnp.moveaxis(inp, 2, 0)
            uc = jnp.moveaxis(_dir_scan(xH, w_up[:-1]), 0, 2)
            dc = jnp.moveaxis(_dir_scan(xH[::-1], w_down[::-1][:-1])[::-1], 0, 2)
            xW = jnp.moveaxis(inp, 3, 0)
            lc = jnp.moveaxis(_dir_scan(xW, w_left.T[:-1]), 0, 3)
            rc = jnp.moveaxis(_dir_scan(xW[::-1], w_right.T[::-1][:-1])[::-1], 0, 3)
            ctx = jnp.concatenate([lc, rc, uc, dc], axis=1)
            out = jnp.einsum('bkhw,ck->bchw', ctx, conv_w) + conv_b[None, :, None, None]
            return jnp.maximum(out, 0.0)
        key = jax.random.key(seed)
        k1, k2, k3, k4 = jax.random.split(key, 4)
        inp = jax.random.normal(k1, (B, C, H, W), dtype=jnp.float32)
        weights = jax.random.normal(k2, (4, H, W), dtype=jnp.float32) * 0.1
        conv_w = jax.random.normal(k3, (C, 4 * C), dtype=jnp.float32) / np.sqrt(4 * C)
        conv_b = jax.random.normal(k4, (C,), dtype=jnp.float32) * 0.01
        return {'inp': inp, 'weights': weights, 'conv_w': conv_w, 'conv_b': conv_b}
    _L1_conv_all = _L1_conv_setup()
    _L1_conv_in = {k: v for k, v in _L1_conv_all.items() if k in ('weights', 'conv_w', 'conv_b', )}
    del _L1_conv_all

    def _L2_conv_setup():
        import jax, jax.numpy as jnp
        import numpy as np
        from jax import lax
        B, C, H, W = (16, 32, 384, 384)
        NK = 32
        K = 3
        HID = 128
        key = jax.random.key(seed)
        ks = jax.random.split(key, 5)
        x = jax.random.normal(ks[0], (B, C, H, W), dtype=jnp.float32)
        w1 = jax.random.normal(ks[1], (C, HID), dtype=jnp.float32) * (1.0 / np.sqrt(C))
        b1 = jnp.zeros((HID,), dtype=jnp.float32)
        w2 = jax.random.normal(ks[2], (HID, NK * K * K), dtype=jnp.float32) * (1.0 / np.sqrt(HID))
        b2 = jnp.zeros((NK * K * K,), dtype=jnp.float32)
        return {'x': x, 'w1': w1, 'b1': b1, 'w2': w2, 'b2': b2}
    _L2_conv_all = _L2_conv_setup()
    _L2_conv_in = {k: v for k, v in _L2_conv_all.items() if k in ('w1', 'b1', 'w2', 'b2', )}
    del _L2_conv_all

    def _L3_conv_setup():
        import jax, jax.numpy as jnp
        import numpy as np
        from jax import lax
        PS = 2
        DN = ('NCHW', 'OIHW', 'NCHW')
        key = jax.random.key(seed)
        ks = jax.random.split(key, 7)
        B, C, H, W = (8, 32, 512, 512)
        return {'x': jax.random.normal(ks[0], (B, C, H, W), dtype=jnp.float32), 'mlp_w': jax.random.normal(ks[1], (1, 1), dtype=jnp.float32), 'mlp_b': jax.random.normal(ks[2], (1,), dtype=jnp.float32) * 0.1, 'conv_w': jax.random.normal(ks[3], (C, 2 * C, 1, 1), dtype=jnp.float32) * (1.0 / np.sqrt(2 * C)), 'conv_b': jax.random.normal(ks[4], (C,), dtype=jnp.float32) * 0.1, 'convout_w': jax.random.normal(ks[5], (C, 2, 7, 7), dtype=jnp.float32) * (1.0 / np.sqrt(2 * 49)), 'convout_b': jax.random.normal(ks[6], (C,), dtype=jnp.float32) * 0.1}
    _L3_conv_all = _L3_conv_setup()
    _L3_conv_in = {k: v for k, v in _L3_conv_all.items() if k in ('mlp_w', 'mlp_b', 'conv_w', 'conv_b', 'convout_w', 'convout_b', )}
    del _L3_conv_all

    return {
        "x": x,
        "L0_conv_coeff_real": _L0_conv_in["coeff_real"],
        "L0_conv_coeff_imag": _L0_conv_in["coeff_imag"],
        "L0_conv_proj": _L0_conv_in["proj"],
        "L1_conv_weights": _L1_conv_in["weights"],
        "L1_conv_conv_w": _L1_conv_in["conv_w"],
        "L1_conv_conv_b": _L1_conv_in["conv_b"],
        "L2_conv_w1": _L2_conv_in["w1"],
        "L2_conv_b1": _L2_conv_in["b1"],
        "L2_conv_w2": _L2_conv_in["w2"],
        "L2_conv_b2": _L2_conv_in["b2"],
        "L3_conv_mlp_w": _L3_conv_in["mlp_w"],
        "L3_conv_mlp_b": _L3_conv_in["mlp_b"],
        "L3_conv_conv_w": _L3_conv_in["conv_w"],
        "L3_conv_conv_b": _L3_conv_in["conv_b"],
        "L3_conv_convout_w": _L3_conv_in["convout_w"],
        "L3_conv_convout_b": _L3_conv_in["convout_b"],
    }

def reference(x, L0_conv_coeff_real, L0_conv_coeff_imag, L0_conv_proj, L1_conv_weights, L1_conv_conv_w, L1_conv_conv_b, L2_conv_w1, L2_conv_b1, L2_conv_w2, L2_conv_b2, L3_conv_mlp_w, L3_conv_mlp_b, L3_conv_conv_w, L3_conv_conv_b, L3_conv_convout_w, L3_conv_convout_b):
    import jax
    import jax.numpy as jnp
    def _L0_conv_ref(x, coeff_real, coeff_imag, proj):
        import jax, jax.numpy as jnp
        import numpy as np
        B, IN_CH, OUT_CH, R = (16, 32, 32, 32)
        M1, M2 = (32, 32)
        H, W = (256, 256)
        x_ft = jnp.fft.rfftn(x, axes=(-2, -1))
        coeff = (coeff_real + 1j * coeff_imag).astype(jnp.complex64)
        Wt = jnp.einsum('or,rabi->oabi', proj.astype(jnp.complex64), coeff)
        Hf, Wf = (x_ft.shape[-2], x_ft.shape[-1])
        m1 = min(M1, Hf)
        m2 = min(M2, Wf)
        sub = jnp.einsum('bcij,ocij->boij', x_ft[..., :m1, :m2], Wt[:, :, :m1, :m2])
        out_ft = jnp.zeros((x.shape[0], OUT_CH, Hf, Wf), jnp.complex64)
        out_ft = out_ft.at[..., :m1, :m2].set(sub.astype(jnp.complex64))
        return jnp.fft.irfftn(out_ft, s=(x.shape[-2], x.shape[-1]), axes=(-2, -1))

    def _L1_conv_ref(inp, weights, conv_w, conv_b):
        import jax, jax.numpy as jnp
        import numpy as np
        B, C, H, W = (16, 32, 256, 256)

        def _dir_scan(xT, w_seq):

            def step(prev, xs):
                xr, wr = xs
                new = jnp.maximum(wr * prev + xr, 0.0)
                return (new, new)
            _, outs = jax.lax.scan(step, xT[0], (xT[1:], w_seq))
            return jnp.concatenate([xT[:1], outs], axis=0)

        def _forward(inp, weights, conv_w, conv_b):
            w_up, w_down, w_left, w_right = jax.nn.sigmoid(weights)
            xH = jnp.moveaxis(inp, 2, 0)
            uc = jnp.moveaxis(_dir_scan(xH, w_up[:-1]), 0, 2)
            dc = jnp.moveaxis(_dir_scan(xH[::-1], w_down[::-1][:-1])[::-1], 0, 2)
            xW = jnp.moveaxis(inp, 3, 0)
            lc = jnp.moveaxis(_dir_scan(xW, w_left.T[:-1]), 0, 3)
            rc = jnp.moveaxis(_dir_scan(xW[::-1], w_right.T[::-1][:-1])[::-1], 0, 3)
            ctx = jnp.concatenate([lc, rc, uc, dc], axis=1)
            out = jnp.einsum('bkhw,ck->bchw', ctx, conv_w) + conv_b[None, :, None, None]
            return jnp.maximum(out, 0.0)
        return _forward(inp, weights, conv_w, conv_b)

    def _L2_conv_ref(x, w1, b1, w2, b2):
        import jax, jax.numpy as jnp
        import numpy as np
        from jax import lax
        B, C, H, W = (16, 32, 384, 384)
        NK = 32
        K = 3
        HID = 128
        b, c, h, w = x.shape
        pooled = x.mean(axis=(2, 3))
        hdn = jax.nn.relu(pooled @ w1 + b1)
        kernels = (hdn @ w2 + b2).reshape(b, NK, K, K)
        xg = x[:, :NK].reshape(1, b * NK, h, w)
        wgt = kernels.reshape(b * NK, 1, K, K)
        pad = K // 2
        out = lax.conv_general_dilated(xg, wgt, window_strides=(1, 1), padding=[(pad, pad), (pad, pad)], feature_group_count=b * NK, dimension_numbers=('NCHW', 'OIHW', 'NCHW'))
        return out.reshape(b, NK, h, w)

    def _L3_conv_ref(x, mlp_w, mlp_b, conv_w, conv_b, convout_w, convout_b):
        import jax, jax.numpy as jnp
        import numpy as np
        from jax import lax
        PS = 2
        DN = ('NCHW', 'OIHW', 'NCHW')
        B, C, H, W = x.shape
        hn, wn = (H // PS, W // PS)
        xb = x.reshape(B, C, hn, PS, wn, PS)
        m = jnp.max(xb, axis=(3, 5))
        a = jnp.mean(xb, axis=(3, 5))
        gate = jax.nn.sigmoid((m + a) * mlp_w[0, 0] + 2.0 * mlp_b[0])
        product = (xb * gate[:, :, :, None, :, None]).reshape(B, C, H, W)
        cat = jnp.concatenate([product, x], axis=1)
        out = lax.conv_general_dilated(cat, conv_w, (1, 1), 'SAME', dimension_numbers=DN) + conv_b[None, :, None, None]
        fs = out
        cm = jnp.max(out, axis=1, keepdims=True)
        ca = jnp.mean(out, axis=1, keepdims=True)
        att = lax.conv_general_dilated(jnp.concatenate([cm, ca], axis=1), convout_w, (1, 1), 'SAME', dimension_numbers=DN)
        att = att + convout_b[None, :, None, None]
        return jax.nn.sigmoid(att) * fs

    def _gn(v, G=16, eps=1e-5):
        B_, C_, H_, W_ = v.shape
        g = v.reshape(B_, G, C_ // G, H_, W_)
        m = jnp.mean(g, axis=(2, 3, 4), keepdims=True)
        s = jnp.var(g, axis=(2, 3, 4), keepdims=True)
        return ((g - m) / jnp.sqrt(s + eps)).reshape(v.shape)

    def _ln_c(v, eps=1e-6):
        m = jnp.mean(v, axis=1, keepdims=True)
        s = jnp.var(v, axis=1, keepdims=True)
        return (v - m) / jnp.sqrt(s + eps)

    def _ln_t(v, eps=1e-5):
        m = jnp.mean(v, axis=-1, keepdims=True)
        s = jnp.var(v, axis=-1, keepdims=True)
        return (v - m) / jnp.sqrt(s + eps)

    def _to_tokens(v):
        B_, C_, H_, W_ = v.shape
        return v.reshape(B_, C_, H_ * W_).transpose(0, 2, 1)
    def _from_tokens(t, like):
        B_, C_, H_, W_ = like.shape
        return t.transpose(0, 2, 1).reshape(B_, C_, H_, W_)

    x = x + _L0_conv_ref(_gn(x), L0_conv_coeff_real, L0_conv_coeff_imag, L0_conv_proj)
    x = x + _L1_conv_ref(_gn(x), L1_conv_weights, L1_conv_conv_w, L1_conv_conv_b)
    x = x + _L2_conv_ref(_gn(x), L2_conv_w1, L2_conv_b1, L2_conv_w2, L2_conv_b2)
    x = x + _L3_conv_ref(_gn(x), L3_conv_mlp_w, L3_conv_mlp_b, L3_conv_conv_w, L3_conv_conv_b, L3_conv_convout_w, L3_conv_convout_b)
    return x


_drawn_inputs = setup_inputs


def setup_inputs(seed=0):
    import zlib

    import numpy as np

    out = dict(_drawn_inputs(seed))
    spreads = {'L2_conv_b1': (0.0, 0.344), 'L2_conv_b2': (0.0, 0.1)}
    factors = {'L1_conv_weights': 8.0,
     'L1_conv_conv_b': 50.189,
     'L2_conv_w1': 6.413,
     'L3_conv_conv_b': 7.339,
     'L3_conv_convout_b': 8.0}
    for name, (base, spread) in spreads.items():
        noise = np.random.default_rng([zlib.crc32(name.encode()), seed]).standard_normal(out[name].shape)
        drawn = base * np.exp(spread * noise) if base else spread * noise
        out[name] = jnp.asarray(drawn.astype(out[name].dtype))
    for name, factor in factors.items():
        out[name] = (out[name] * factor).astype(out[name].dtype)
    return out
```

```python
from contextlib import ExitStack

import numpy as np

import concourse.bass as bass
from concourse import mybir

F32 = mybir.dt.float32
ALU = mybir.AluOpType
ACT = mybir.ActivationFunctionType
AX = mybir.AxisListType

P = 128
C = 32
H = W = 256
Q = P // C
QR = H // Q
HW = H * W
G = 16
M1 = M2 = 32
J = 4
NG = M1 // J
EPS = 1e-5
MAPW = 264
PAD = 3


class Chain:

    def __init__(self, eng, sem, base=0):
        self.eng, self.sem, self.base, self.n = eng, sem, base, 0

    def then(self, ins):
        self.n += 1
        ins.then_inc(self.sem, 1)
        self.eng.wait_ge(self.sem, self.base + self.n)


def phase_sem(nc, mem, name):
    handle = nc.alloc_semaphore(name=name)
    mem.sems.append(handle)
    return handle


def wait_alone(eng, sem, value, passed):
    eng.wait_ge(sem, value)
    eng.sem_inc(passed, 1)


class Phase(ExitStack):

    def __init__(self, nc):
        super().__init__()
        self.nc, self.sems = nc, []

    def __exit__(self, *exc):
        if exc[0] is None:
            self.nc.clear_and_free_semaphores(self.sems)
            self.nc.all_engine_barrier()
        return super().__exit__(*exc)


def loads(eng, sem, pairs):
    for dst, src in pairs:
        eng.dma_start(dst, src).then_inc(sem, 16)
    eng.wait_ge(sem, 16 * len(pairs))


def rstd_of(nc, eng, chain, act_sem, back_sem, var, out, tmp):
    chain.then(eng.tensor_scalar(var, var, EPS, None, ALU.add))
    eng.sem_inc(act_sem, 1)
    eng.wait_ge(back_sem, 1)
    chain.then(eng.reciprocal(out, tmp))
    chain.then(eng.tensor_tensor(tmp, out, out, ALU.mult))
    chain.then(eng.tensor_tensor(tmp, tmp, var, ALU.mult))
    chain.then(eng.tensor_scalar(tmp, tmp, -0.5, 1.5, ALU.mult, ALU.add))
    chain.then(eng.tensor_tensor(out, out, tmp, ALU.mult))


def setup_phase(nc, top, io, gates, maps, x2_guard, t):
    with Phase(nc) as mem:
        sb = lambda n, s: mem.enter_context(nc.sbuf_tensor(n, s, F32))
        raw = sb("gate_raw", [P, 4, 2, H])
        sig = sb("gate_sig", [P, 4, 2, H])
        zero = sb("zero_rows", [P, 4096])
        wd, wm = sb("wd", [P, 4, C]), sb("wm", [P, 2, C])
        s = {n: phase_sem(nc, mem, ("set_" + n)) for n in
             ("raw", "small", "zeroed", "wide", "sig", "out", "neg")}
        with nc.Block() as block:
            @block.sync
            def _(sp):
                sp.dma_start(raw[:, :, :, :], io["scan_w"].rearrange("d (p l) k -> p d l k", p=P)).then_inc(s["raw"], 16)
                n = 6
                for dst, src, m in ((wd, "conv1_T", 4), (wm, "conv3_T", 2)):
                    for i in range(m):
                        sp.dma_start(dst[:, i, :], bass.AP(io[src].tensor, i * C * C, [[C, C], [0, Q], [1, C]])).then_inc(s["small"], 16)
                for name, src in (("bias1", "conv1_b"), ("bias3", "conv3_b"), ("bias_att", "att_b")):
                    sp.dma_start(t[name][:, :], bass.AP(io[src].tensor, 0, [[1, C], [0, Q], [1, 1]])).then_inc(s["small"], 16)
                    n += 1
                for k, name in enumerate(("mlp_w", "mlp_b")):
                    sp.dma_start(t["mlp"][:, k:k + 1], bass.AP(io[name].tensor, 0, [[0, P], [1, 1]])).then_inc(s["small"], 16)
                    n += 1
                for name in ("ident", "group_avg", "mask_cq", "mask_jc", "chan_mean", "quarter"):
                    sp.dma_start(t[name][:, :], io[name]).then_inc(s["small"], 16)
                    n += 1
                sp.wait_ge(s["small"], 16 * n)
                sp.wait_ge(s["zeroed"], 1)
                sp.wait_ge(s["sig"], 1)
                sp.dma_start(gates.rearrange("d (p l) k -> p d l k", p=P), sig[:, :, :, :]).then_inc(s["out"], 16)
                sp.dma_start(x2_guard, zero[0:2, 0:W]).then_inc(s["out"], 16)
                n_out = 2
                per = MAPW * 2 * MAPW
                for b in range(maps.shape[0]):
                    flat = bass.AP(maps.tensor, b * per, [[per // 96, 96], [1, per // 96]])
                    sp.dma_start(flat, zero[0:96, 0:per // 96]).then_inc(s["out"], 16)
                    n_out += 1
                sp.wait_ge(s["out"], 16 * n_out)

            @block.vector
            def _(dve):
                dve.memset(zero[:, :], 0.0).then_inc(s["zeroed"], 1)
                dve.memset(sig[:, :, :, :], 0.0).then_inc(s["zeroed"], 1)
                dve.wait_ge(s["small"], 16 * 17)
                for k, (dst, src, m) in enumerate(((t["w_dir"], wd, 4), (t["w_mix"], wm, 2))):
                    for i in range(m):
                        dve.tensor_tensor(dst[:, i, :].rearrange("p (o q) -> p o q", q=Q),
                                          src[:, i, :].unsqueeze(2).to_broadcast([P, C, Q]),
                                          t["quarter"][:, :].unsqueeze(1).to_broadcast([P, C, Q]), ALU.mult).then_inc(s["wide"], 1)
                dve.wait_ge(s["wide"], 6)
                dve.tensor_scalar(t["w_neg"][:, :, :], t["w_dir"][:, :, :], -1.0, None, ALU.mult).then_inc(s["neg"], 1)
                dve.tensor_scalar(t["mlp"][:, 1:2], t["mlp"][:, 1:2], 2.0, None, ALU.mult).then_inc(s["neg"], 1)

            @block.scalar
            def _(act):
                act.wait_ge(s["raw"], 16)
                act.wait_ge(s["zeroed"], 2)
                for i in range(4):
                    fwd = i % 2 == 0
                    dst = sig[:, i, :, 1:H] if fwd else sig[:, i, :, 0:H - 1]
                    src = raw[:, i, :, 0:H - 1] if fwd else raw[:, i, :, 1:H]
                    last = act.activation(dst, src, ACT.Sigmoid)
                last.then_inc(s["sig"], 1)


def stats_from_rows(nc, top, tag, NB, bn, mask, norm):
    E = NB * C * 2
    with Phase(nc) as mem:
        sb = lambda n, s: mem.enter_context(nc.sbuf_tensor(tag + n, s, F32))
        ones = sb("ones", [P, P])
        dev = sb("dev", [P, E])
        mg, vg, rg, tg = (sb(n, [P, NB * G]) for n in ("mg", "vg", "rg", "tg"))
        spread = sb("spread", [P, 2, NB, G])
        ps = mem.enter_context(nc.psum_tensor(tag + "ps", [P, E], F32))
        s = {n: phase_sem(nc, mem, (tag + n)) for n in ("dve", "mm", "feed", "root", "rooted")}
        entry = bn.rearrange("p b c (e s) -> p (b c e) s", s=3)
        mean_i, m2_i = entry[:, :, 1], entry[:, :, 2]
        with nc.Block() as block:
            @block.vector
            def _(dve):
                ch = Chain(dve, s["dve"])
                ch.then(dve.memset(ones[:, :], 1.0 / (P * 4)))
                dve.sem_inc(s["feed"], 1)
                dve.wait_ge(s["mm"], 1)
                ch.then(dve.tensor_reduce(mg[:, :], ps[:, :].rearrange("p (g e) -> p g e", e=4), AX.X, ALU.add))
                ch.then(dve.tensor_tensor(dev[:, :].rearrange("p (g e) -> p g e", e=4),
                                          mean_i.rearrange("p (g e) -> p g e", e=4),
                                          mg[:, :].unsqueeze(2).to_broadcast([P, NB * G, 4]), ALU.subtract))
                ch.then(dve.tensor_tensor(dev[:, :], dev[:, :], dev[:, :], ALU.mult))
                ch.then(dve.scalar_tensor_tensor(dev[:, :], m2_i, 1.0 / W, dev[:, :], ALU.mult, ALU.add))
                dve.sem_inc(s["feed"], 1)
                dve.wait_ge(s["mm"], 2)
                ch.then(dve.tensor_reduce(vg[:, :], ps[:, :].rearrange("p (g e) -> p g e", e=4), AX.X, ALU.add))
                rstd_of(nc, dve, ch, s["root"], s["rooted"], vg[:, :], rg[:, :], tg[:, :])
                for k, v in enumerate((rg, mg)):
                    ch.then(dve.tensor_tensor(spread[:, k, :, :], v[:, :].rearrange("p (b g) -> p b g", g=G),
                                              mask.unsqueeze(1).to_broadcast([P, NB, G]), ALU.mult))
                ch.then(dve.tensor_reduce(norm[:, :, 0], spread[:, 0, :, :], AX.X, ALU.add))
                ch.then(dve.tensor_reduce(norm[:, :, 2], spread[:, 1, :, :], AX.X, ALU.add))
                ch.then(dve.scalar_tensor_tensor(norm[:, :, 1], norm[:, :, 0], -1.0, norm[:, :, 2], ALU.mult, ALU.mult))

            @block.tensor
            def _(pe):
                for k in range(2):
                    pe.wait_ge(s["feed"], k + 1)
                    src = mean_i if k == 0 else dev[:, :]
                    for n in range(0, E, 512):
                        m = min(512, E - n)
                        last = nc.tensor.matmul(ps[:, n:n + m], ones[:, :], src[:, n:n + m], start=True, stop=True)
                    last.then_inc(s["mm"], 1)

            @block.scalar
            def _(act):
                act.wait_ge(s["root"], 1)
                act.activation(tg[:, :], vg[:, :], ACT.Sqrt).then_inc(s["rooted"], 1)


def stats_from_quarters(nc, top, tag, NB, mv, t, norm, w_pool=None):
    with Phase(nc) as mem:
        sb = lambda n, s: mem.enter_context(nc.sbuf_tensor(tag + n, s, F32))
        dev = sb("dev", [P, NB])
        var, rs, tmp = sb("var", [P, NB]), sb("rs", [P, NB]), sb("tmp", [P, NB])
        ps = mem.enter_context(nc.psum_tensor(tag + "ps", [P, 2, 512], F32))
        s = {n: phase_sem(nc, mem, (tag + n)) for n in ("dve", "mm", "feed", "root", "rooted")}
        with nc.Block() as block:
            @block.vector
            def _(dve):
                ch = Chain(dve, s["dve"])
                dve.wait_ge(s["mm"], 1)
                ch.then(dve.tensor_copy(norm[:, :, 2], ps[:, 0, 0:NB]))
                ch.then(dve.tensor_tensor(dev[:, :], mv[:, :, 0], norm[:, :, 2], ALU.subtract))
                ch.then(dve.tensor_tensor(dev[:, :], dev[:, :], dev[:, :], ALU.mult))
                ch.then(dve.tensor_tensor(dev[:, :], dev[:, :], mv[:, :, 1], ALU.add))
                dve.sem_inc(s["feed"], 1)
                dve.wait_ge(s["mm"], 2)
                ch.then(dve.tensor_copy(var[:, :], ps[:, 1, 0:NB]))
                rstd_of(nc, dve, ch, s["root"], s["rooted"], var[:, :], rs[:, :], tmp[:, :])
                ch.then(dve.tensor_copy(norm[:, :, 0], rs[:, :]))
                ch.then(dve.scalar_tensor_tensor(norm[:, :, 1], rs[:, :], -1.0, norm[:, :, 2], ALU.mult, ALU.mult))

            @block.tensor
            def _(pe):
                nc.tensor.matmul(ps[:, 0, 0:NB], t["group_avg"][:, :], mv[:, :, 0], start=True, stop=True).then_inc(s["mm"], 1)
                pe.wait_ge(s["feed"], 1)
                nc.tensor.matmul(ps[:, 1, 0:NB], t["group_avg"][:, :], dev[:, :], start=True, stop=True).then_inc(s["mm"], 1)

            @block.scalar
            def _(act):
                act.wait_ge(s["root"], 1)
                act.activation(tmp[:, :], var[:, :], ACT.Sqrt).then_inc(s["rooted"], 1)


CG = 8
NCG = C // CG


def spectrum_phase(nc, top, NB, x, io, bn, X):
    with Phase(nc) as mem:
        sb = lambda n, s: mem.enter_context(nc.sbuf_tensor("sp_" + n, s, F32))
        NS = 3
        xin = sb("xin", [P, 4, 2, CG, W])
        fh = sb("fh", [P, 2, 64])
        fw = sb("fw", [P, 2, 2, 64])
        A = sb("A", [P, 2, 2, M1, C])
        psA = mem.enter_context(nc.psum_tensor("sp_psA", [P, 2, 2, CG * 64], F32))
        psX = mem.enter_context(nc.psum_tensor("sp_psX", [P, NG * 64], F32))
        sem = lambda n: phase_sem(nc, mem, ("sp_" + n))
        small = sem("small")
        x_full = [sem(f"x_full{i}") for i in range(4)]
        x_free_pe, x_free_dve = sem("x_free_pe"), sem("x_free_dve")
        a_ready, a_copied, x_ready, x_copied = sem("a_ready"), sem("a_copied"), sem("x_ready"), sem("x_copied")
        with nc.Block() as block:
            @block.sync
            def _(sp):
                loads(sp, small, [(fh[:, :, :], io["dft_h"].rearrange("(t p) k -> p t k", p=P)),
                                  (fw[:, :, :, :], io["dft_w"].rearrange("(t p) a k -> p t a k", p=P))])
                with sp.Fori(0, NB) as b:
                    for k in range(NCG):
                        sp.wait_ge(x_free_pe, b * NCG + k + 1)
                        sp.wait_ge(x_free_dve, b * NCG + k + 1)
                        for h in range(2):
                            sp.dma_start(xin[:, k, h, :, :],
                                         x[b, k * CG:(k + 1) * CG, h * P:(h + 1) * P, :].rearrange("c p w -> p c w")
                                         ).then_inc(x_full[k], 16)

            @block.tensor
            def _(pe):
                pe.wait_ge(small, 32)
                pe.sem_inc(x_free_pe, 4)
                pe.sem_inc(x_ready, 1)
                with pe.Fori(0, NB) as b:
                    for k in range(NCG):
                        pe.wait_ge(x_full[k], 32 * b + 32)
                        pe.wait_ge(a_copied, b * NCG + k + 1)
                        for wh in range(2):
                            for c in range(CG):
                                for h in range(2):
                                    last = nc.tensor.matmul(psA[:, k % 2, wh, c * 64:(c + 1) * 64],
                                                            xin[:, k, h, c, wh * P:(wh + 1) * P], fh[:, h, :],
                                                            start=(h == 0), stop=(h == 1))
                        last.then_inc(a_ready, 1)
                        pe.wait_ge(a_ready, b * NCG + k + 1)
                        pe.sem_inc(x_free_pe, 1)
                    pe.wait_ge(a_copied, b * NCG + NCG + 2)
                    pe.wait_ge(x_copied, b + 1)
                    for g in range(NG):
                        n = 0
                        for wh in range(2):
                            for cs in range(2):
                                last = nc.tensor.matmul(psX[:, g * 64:(g + 1) * 64],
                                                        A[:, wh, cs, g * J:(g + 1) * J, :].rearrange("p j c -> p (j c)"),
                                                        fw[:, wh, cs, :], start=(n == 0), stop=(n == 3))
                                n += 1
                    last.then_inc(x_ready, 1)

            @block.scalar
            def _(act):
                act.sem_inc(a_copied, 2)
                act.sem_inc(x_copied, 1)
                with act.Fori(0, NB) as b:
                    act.wait_ge(x_ready, b + 1)
                    for k in range(NCG):
                        act.wait_ge(a_ready, b * NCG + k + 1)
                        for wh in range(2):
                            last = act.activation(A[:, wh, :, :, k * CG:(k + 1) * CG].rearrange("p a k c -> p c (a k)"),
                                                  psA[:, k % 2, wh, :].rearrange("p (c n) -> p c n", c=CG), ACT.Copy)
                        last.then_inc(a_copied, 1)
                    act.wait_ge(x_ready, b + 2)
                    act.activation(X[:, b, :], psX[:, :], ACT.Copy).then_inc(x_copied, 1)

            @block.vector
            def _(dve):
                dve.sem_inc(x_free_dve, 4)
                with dve.Fori(0, NB) as b:
                    for k in range(NCG):
                        dve.wait_ge(x_full[k], 32 * b + 32)
                        for c in range(CG):
                            last = dve.bn_stats(bn[:, b, k * CG + c, :], xin[:, k, :, c, :])
                        last.then_inc(x_free_dve, 1)


def mixing_phase(nc, top, NB, io, X, norm, Y):
    with Phase(nc) as mem:
        sb = lambda n, s: mem.enter_context(nc.sbuf_tensor("mx_" + n, s, F32))
        coef = sb("coef", [C, 2, 2, M2, J, C])
        proj = sb("proj", [C, 4, C])
        W3 = sb("W3", [P, M2, 3, C])
        Xg = sb("Xg", [P, 2, NB, 64])
        Yg = sb("Yg", [NB, 64, J, M2])
        psW = mem.enter_context(nc.psum_tensor("mx_psW", [P, 4, 4, 128], F32))
        psY = mem.enter_context(nc.psum_tensor("mx_psY", [NB, 4, 8, 64], F32))
        sem = lambda n: phase_sem(nc, mem, ("mx_" + n))
        small, c_full = sem("small"), [sem(f"c_full{i}") for i in range(2)]
        prep, w_ready, w_copied, c_free, g_ready = sem("prep"), sem("w_ready"), sem("w_copied"), sem("c_free"), sem("g_ready")
        y_ready, y_copied, mixed, stored, w3_done = sem("y_ready"), sem("y_copied"), sem("mixed"), sem("stored"), sem("w3_done")
        QUADS = M2 // 4
        with nc.Block() as block:
            @block.sync
            def _(sp):
                loads(sp, small, [(proj[:, i, :], io["proj_T"]) for i in range(4)])
                for g in range(NG):
                    if g >= 2:
                        sp.wait_ge(c_free, g - 1)
                    for a, n in enumerate(("coeff_real", "coeff_imag")):
                        sp.dma_start(coef[:, g % 2, a, :, :, :], io[n][:, g, :, :, :]).then_inc(c_full[g % 2], 16)
                    if g >= 1:
                        sp.wait_ge(y_copied, 4 * g)
                        for j in range(J):
                            sp.dma_start(Y[:, :, :, (g - 1) * J + j, :].rearrange("b a o k -> b (a o) k"),
                                         Yg[:, :, j, :]).then_inc(stored, 16)
                sp.wait_ge(y_copied, 4 * NG)
                for j in range(J):
                    sp.dma_start(Y[:, :, :, (NG - 1) * J + j, :].rearrange("b a o k -> b (a o) k"),
                                 Yg[:, :, j, :]).then_inc(stored, 16)
                sp.wait_ge(stored, 16 * J * NG)

            @block.vector
            def _(dve):
                ch = Chain(dve, prep)
                dve.wait_ge(small, 64)
                ch.then(dve.tensor_scalar(proj[:, 0, :], proj[:, 0, :], -1.0, None, ALU.mult))
                nrm = norm
                ch.then(dve.scalar_tensor_tensor(X[0:C, :, 0], nrm[0:C, :, 2], -float(HW), X[0:C, :, 0], ALU.mult, ALU.add))
                for g in range(NG):
                    if g >= 2:
                        dve.wait_ge(mixed, 4 * (g - 1))
                    ch.then(dve.tensor_tensor(Xg[:, g % 2, :, :], X[:, :, g * 64:(g + 1) * 64],
                                              nrm[:, :, 0].unsqueeze(2).to_broadcast([P, NB, 64]), ALU.mult))
                    dve.sem_inc(g_ready, 1)
                    if g >= 1:
                        dve.wait_ge(mixed, 4 * g)
                    for n in range(QUADS):
                        dve.wait_ge(w_ready, g * QUADS + n + 1)
                        dve.tensor_copy(W3[:, 4 * n:4 * n + 4, :, :].rearrange("p k a o -> p k (a o)"),
                                        psW[:, n % 4, :, 0:96]).then_inc(w_copied, 1)

            @block.tensor
            def _(pe):
                pe.wait_ge(prep, 1)
                for g in range(NG):
                    pe.wait_ge(c_full[g % 2], 32 * (g // 2 + 1))
                    for n in range(QUADS):
                        m = g * QUADS + n
                        if m >= 4:
                            pe.wait_ge(w_copied, m - 3)
                        for i in range(4):
                            k2 = 4 * n + i
                            for v in range(2):
                                out = psW[:, n % 4, i, :].rearrange("p (o v c) -> p v o c", v=2, c=C)[:, 1 - v, :, :]
                                last = nc.tensor.matmul(out, coef[:, g % 2, v, k2, :, :].rearrange("p j c -> p (j c)"),
                                                        proj[:, 2 - 2 * v:4 - 2 * v, :].rearrange("p a o -> p (a o)"), start=True, stop=True)
                        last.then_inc(w_ready, 1)
                    pe.wait_ge(w_ready, (g + 1) * QUADS)
                    pe.sem_inc(c_free, 1)
                    pe.wait_ge(w_copied, (g + 1) * QUADS)
                    pe.wait_ge(g_ready, g + 1)
                    for e in range(4):
                        if 4 * g + e >= 1:
                            pe.wait_ge(y_copied, 4 * g + e)
                        for i in range(8):
                            k2 = 8 * e + i
                            for j in range(J):
                                r = slice(C * j, C * j + C)
                                nc.tensor.matmul(psY[:, j, i, :], Xg[r, g % 2, :, k2],
                                                 W3[r, k2, 1:3, :].rearrange("p a o -> p (a o)"), start=True, stop=False)
                                last = nc.tensor.matmul(psY[:, j, i, :], Xg[r, g % 2, :, 32 + k2],
                                                        W3[r, k2, 0:2, :].rearrange("p a o -> p (a o)"), start=False, stop=True)
                        last.then_inc(mixed, 1)

            @block.scalar
            def _(act):
                for g in range(NG):
                    if g >= 1:
                        act.wait_ge(stored, 16 * J * g)
                    for e in range(4):
                        act.wait_ge(mixed, 4 * g + e + 1)
                        for j in range(J):
                            last = act.activation(Yg[:, :, j, 8 * e:8 * e + 8].rearrange("b o k -> b k o"),
                                                  psY[:, j, :, :], ACT.Copy)
                        last.then_inc(y_copied, 1)


def inverse_phase(nc, top, NB, x, io, Y, x1, bn):
    with Phase(nc) as mem:
        sb = lambda n, s: mem.enter_context(nc.sbuf_tensor("iv_" + n, s, F32))
        xin = sb("xin", [P, 4, CG, 2, W])
        Yb = sb("Yb", [64, C, 2, M2])
        Z = sb("Z", [P, C // 2, H])
        eh = sb("eh", [64, H])
        fw = sb("fw", [P, 2, W])
        psZ = mem.enter_context(nc.psum_tensor("iv_psZ", [P, 2, 2, H], F32))
        psI = mem.enter_context(nc.psum_tensor("iv_psI", [P, 4, 2, W], F32))
        sem = lambda n: phase_sem(nc, mem, ("iv_" + n))
        passed = sem("passed")
        small = sem("small")
        x_full, x_out, x_free = [sem(f"x_full{i}") for i in range(4)], sem("x_out"), sem("x_free")
        y_full = sem("y_full")
        y_neg, z_ready, z_copied, i_ready, added, x_done = sem("y_neg"), sem("z_ready"), sem("z_copied"), sem("i_ready"), sem("added"), sem("x_done")
        with nc.Block() as block:
            @block.sync
            def _(sp):
                loads(sp, small, [(eh[:, :], io["idft_h"]), (fw[:, :, :], io["idft_w"].rearrange("p (a w) -> p a w", a=2))])
                with sp.Fori(0, NB) as b:
                    sp.wait_ge(z_ready, b * 8 + 1)
                    for a in range(2):
                        for v in range(2):
                            row = (a ^ v) * 32
                            sp.dma_start(Yb[row:row + 32, :, v, :], Y[b, a].rearrange("o k l -> k o l")).then_inc(y_full, 16)
                    for k in range(NCG):
                        sp.wait_ge(x_free, b * NCG + k + 1)
                        for h in range(2):
                            sp.dma_start(xin[:, k, :, h, :],
                                         x[b, k * CG:(k + 1) * CG, h * P:(h + 1) * P, :].rearrange("c p w -> p c w")
                                         ).then_inc(x_full[k], 16)

            @block.gpsimd
            def _(pool):
                pool.sem_inc(x_free, 4)
                with pool.Fori(0, NB) as b:
                    for k in range(NCG):
                        wait_alone(pool, x_done, b * NCG + k + 1, passed)
                        for h in range(2):
                            pool.dma_start(x1[b, k * CG:(k + 1) * CG, h * P:(h + 1) * P, :].rearrange("c p w -> p c w"),
                                           xin[:, k, :, h, :]).then_inc(x_out, 16)
                        pool.wait_ge(x_out, (b * NCG + k) * 32 + 32)
                        pool.sem_inc(x_free, 1)

            @block.tensor
            def _(pe):
                pe.wait_ge(small, 32)
                pe.sem_inc(z_ready, 1)
                pe.sem_inc(i_ready, 1)
                with pe.Fori(0, NB) as b:
                    pe.wait_ge(y_neg, b + 1)
                    for n in range(8):
                        pe.wait_ge(z_copied, b * 8 + n + 1)
                        for i in range(2):
                            op = 2 * n + i
                            last = nc.tensor.matmul(psZ[:, n % 2, i, :], Yb[:, 2 * op:2 * op + 2, :, :].rearrange("p o v k -> p (o v k)"),
                                                    eh[:, :], start=True, stop=True)
                        last.then_inc(z_ready, 1)
                    pe.wait_ge(z_copied, b * 8 + 10)
                    for op in range(C // 2):
                        pe.wait_ge(added, b * 16 + op + 1)
                        for h in range(2):
                            last = nc.tensor.matmul(psI[:, (2 * op) % 4 + h, :, :].rearrange("p o w -> p (o w)"), Z[:, op, h * P:(h + 1) * P],
                                                    fw[:, :, :].rearrange("p o w -> p (o w)"), start=True, stop=True)
                        last.then_inc(i_ready, 1)

            @block.scalar
            def _(act):
                act.sem_inc(z_copied, 2)
                with act.Fori(0, NB) as b:
                    act.wait_ge(i_ready, b * 16 + 1)
                    for n in range(8):
                        act.wait_ge(z_ready, b * 8 + n + 2)
                        act.activation(Z[:, 2 * n:2 * n + 2, :], psZ[:, n % 2, :, :], ACT.Copy).then_inc(z_copied, 1)

            @block.vector
            def _(dve):
                dve.sem_inc(added, 2)
                with dve.Fori(0, NB) as b:
                    dve.wait_ge(y_full, 64 * b + 64)
                    dve.tensor_scalar(Yb[32:64, :, 0, :], Yb[32:64, :, 0, :], -1.0, None, ALU.mult).then_inc(y_neg, 1)
                    for k in range(NCG):
                        dve.wait_ge(x_full[k], 32 * b + 32)
                        for i in range(CG // 2):
                            op = k * (CG // 2) + i
                            dve.wait_ge(i_ready, b * 16 + op + 2)
                            bank = (2 * op) % 4
                            xs = xin[:, k, 2 * i:2 * i + 2, :, :]
                            dve.tensor_tensor(xs, xs, psI[:, bank:bank + 2, :, :].rearrange("p h c w -> p c h w"), ALU.add).then_inc(added, 1)
                        dve.wait_ge(added, b * 16 + (k + 1) * (CG // 2) + 2)
                        for c in range(CG):
                            last = dve.bn_stats(bn[:, b, k * CG + c, :], xin[:, k, c, :, :])
                        last.then_inc(x_done, 1)


LN = 4
LE = LN * W
NCH = QR // LN


def scan_chunk(dve, n, xn, gate, S, M, step):
    fwd, bwd = slice(None), slice(None, None, -1)
    flat = lambda a, r: a[:, r]
    for d, r in ((0, fwd), (1, bwd)):
        dve.tensor_tensor_scan(flat(S[:, d, :], r), flat(gate[d], r), flat(xn, r), 0.0, ALU.mult, ALU.add).then_inc(step, 1)
    for d, at in ((0, 0), (1, W - 1)):
        dve.wait_ge(step, n * 8 + 1 + d)
        dve.memset(S[:, d, :].rearrange("p (l k) -> p l k", k=W)[:, :, at:at + 1], 0.0).then_inc(step, 1)
    for d, r in ((0, fwd), (1, bwd)):
        dve.wait_ge(step, n * 8 + 3 + d)
        last = dve.tensor_tensor_scan(flat(M[:, d, :], r), flat(gate[d], r), flat(S[:, d, :], r), 0.0, ALU.mult, ALU.min)
        last.then_inc(step, 1)
    for d, at in ((0, 0), (1, W - 1)):
        dve.wait_ge(step, n * 8 + 5 + d)
        first = lambda a: a.rearrange("p (l k) -> p l k", k=W)[:, :, at:at + 1]
        dve.tensor_copy(first(S[:, d, :]), first(xn)).then_inc(step, 1)


def mix_directions(nc, ps, S, M, w_pos, w_neg, first, extra=None):
    for k in range(LE // 512):
        e = slice(k * 512, (k + 1) * 512)
        out = ps[:, k, :]
        if extra is not None:
            nc.tensor.matmul(out, extra[0], extra[1][:, e], start=True, stop=False)
        for d in range(2):
            nc.tensor.matmul(out, w_pos[:, first + d, :], S[:, d, e], start=(d == 0 and extra is None), stop=False)
            last = nc.tensor.matmul(out, w_neg[:, first + d, :], M[:, d, e], start=False, stop=(d == 1))
    return last


def vertical_phase(nc, top, NB, x1, gates, t, norm, pb):
    with Phase(nc) as mem:
        sb = lambda n, s: mem.enter_context(nc.sbuf_tensor("ve_" + n, s, F32))
        img = sb("img", [P, 2, H, QR])
        xn, gt = sb("xn", [P, 2, LE]), sb("gate", [P, 4, 2, LE])
        S, M = sb("S", [P, 2, 2, LE]), sb("M", [P, 2, 2, LE])
        coef = sb("coef", [P, 2, 3])
        ps = mem.enter_context(nc.psum_tensor("ve_ps", [P, 4, 2, 512], F32))
        sem = lambda n: phase_sem(nc, mem, ("ve_" + n))
        img_full, img_out = [sem(f"img_full{i}") for i in range(2)], [sem(f"img_out{i}") for i in range(2)]
        gate_full = [sem(f"gate_full{i}") for i in range(4)]
        coef_ready, xn_ready, step, mixed, evac = sem("coef_ready"), sem("xn_ready"), sem("step"), sem("mixed"), sem("evac")
        
        def move(sp, b, u, store, sem):
            for q in range(Q):
                dram = (pb if store else x1)[b, :, :, q * QR:(q + 1) * QR]
                tile = img[q:q + P - Q + 1:Q, u, :, :]
                sp.dma_start(dram if store else tile, tile if store else dram).then_inc(sem, 16)

        with nc.Block() as block:
            @block.sync
            def _(sp):
                for u in range(2):
                    move(sp, u, u, False, img_full[u])

                def finish(b, u, load):
                    sp.wait_ge(evac, b * NCH + NCH + 4)
                    move(sp, b, u, True, img_out[u])
                    if load:
                        sp.wait_ge(img_out[u], b * 32 + (64 - 32 * u))
                        move(sp, b + 2, u, False, img_full[u])

                if NB > 2:
                    with sp.Fori(0, NB // 2 - 1) as pair:
                        for u in range(2):
                            finish(pair * 2 + u, u, True)
                for u in range(2):
                    finish(NB - 2 + u, u, False)
                for u in range(2):
                    sp.wait_ge(img_out[u], 64 * (NB // 2))
                    sp.wait_ge(gate_full[u], 32 * (NB * NCH // 4 + 1))

            @block.scalar
            def _(act):
                act.sem_inc(evac, 4)

                def load_gates(slot, k):
                    for d in range(2):
                        act.dma_start(gt[:, slot, d, :],
                                      bass.AP(gates.tensor, (2 + d) * HW + k * LE, [[0, C], [HW // Q, Q], [1, LE]])
                                      ).then_inc(gate_full[slot], 16)

                for k in range(2):
                    load_gates(k, k)
                with act.Fori(0, NB // 2) as pair:
                    for u in range(2):
                        b = pair * 2 + u
                        act.wait_ge(mixed, b * NCH + 2)
                        act.activation(coef[:, u, :], norm[:, b, :], ACT.Copy).then_inc(coef_ready, 1)
                        act.wait_ge(coef_ready, b + 1)
                        act.wait_ge(img_full[u], b * 32 + (64 - 32 * u))
                        for k in range(NCH + 2):
                            if k < NCH:
                                n = b * NCH + k
                                act.wait_ge(mixed, n + 1)
                                load_gates((k + 2) % 4, (k + 2) % NCH)
                                act.activation(xn[:, k % 2, :].rearrange("p (l r) -> p l r", r=H),
                                               img[:, u, :, k * LN:(k + 1) * LN].rearrange("p h l -> p l h"),
                                               ACT.Identity, scale=coef[:, u, 0:1], bias=coef[:, u, 1:2]).then_inc(xn_ready, 1)
                            if k >= 2:
                                j = k - 2
                                act.wait_ge(mixed, b * NCH + j + 3)
                                act.activation(img[:, u, :, j * LN:(j + 1) * LN].rearrange("p h l -> p l h"),
                                               ps[:, j % 4, :, :].rearrange("p k (l r) -> p (k l) r", r=H), ACT.Copy).then_inc(evac, 1)

            @block.vector
            def _(dve):
                with dve.Fori(0, NB // 2) as pair:
                    for k in range(2 * NCH):
                        n = pair * (2 * NCH) + k
                        dve.wait_ge(xn_ready, n + 1)
                        dve.wait_ge(gate_full[k % 4], pair * (16 * NCH) + 32 * (k // 4 + 1))
                        dve.wait_ge(mixed, n + 1)
                        scan_chunk(dve, n, xn[:, k % 2, :], [gt[:, k % 4, d, :] for d in range(2)],
                                   S[:, k % 2, :, :], M[:, k % 2, :, :], step)

            @block.tensor
            def _(pe):
                pe.sem_inc(mixed, 2)
                with pe.Fori(0, NB) as b:
                    for k in range(NCH):
                        n = b * NCH + k
                        pe.wait_ge(step, n * 8 + 8)
                        pe.wait_ge(evac, n + 1)
                        mix_directions(nc, ps[:, k % 4, :, :], S[:, k % 2, :, :], M[:, k % 2, :, :],
                                       t["w_dir"], t["w_neg"], 2).then_inc(mixed, 1)


def horizontal_phase(nc, top, NB, x1, pb, gates, t, norm, x2, mv):
    with Phase(nc) as mem:
        sb = lambda n, s: mem.enter_context(nc.sbuf_tensor("ho_" + n, s, F32))
        gt = sb("gate", [P, 2, HW // Q])
        x_in, pb_in = sb("x_in", [P, 4, LE]), sb("pb_in", [P, 2, LE])
        xn, y = sb("xn", [P, 2, LE]), sb("y", [P, 2, LE])
        S, M = sb("S", [P, 2, 2, LE]), sb("M", [P, 2, 2, LE])
        coef = sb("coef", [P, 3])
        bns = sb("bns", [P, 2 * NCH, 6])
        agg = sb("agg", [P, 2])
        ps = mem.enter_context(nc.psum_tensor("ho_ps", [P, 4, 2, 512], F32))
        sem = lambda n: phase_sem(nc, mem, ("ho_" + n))
        passed = sem("passed")
        gate_full, coef_ready = sem("gate_full"), sem("coef_ready")
        x_full, pb_full = [sem(f"x_full{i}") for i in range(4)], [sem(f"pb_full{i}") for i in range(2)]
        y_out, y_free = sem("y_out"), sem("y_free")
        xn_ready, step, mixed, evac, added, stat, agg_done = (sem("xn_ready"), sem("step"), sem("mixed"), sem("evac"), sem("added"), sem("stat"), sem("agg"))
        part = lambda a, b, k: a[b].rearrange("c (q r) w -> (c q) (r w)", q=Q)[:, k * LE:(k + 1) * LE]
        with nc.Block() as block:
            @block.sync
            def _(sp):
                for d in range(2):
                    sp.dma_start(gt[:, d, :], bass.AP(gates.tensor, d * HW, [[0, C], [HW // Q, Q], [1, HW // Q]])).then_inc(gate_full, 16)
                with sp.Fori(0, NB) as b:
                    for k in range(NCH):
                        sp.wait_ge(stat, b * NCH + k + 1)
                        sp.dma_start(x_in[:, k % 4, :], part(x1, b, k)).then_inc(x_full[k % 4], 16)
                        sp.wait_ge(mixed, b * NCH + k + 1)
                        sp.dma_start(pb_in[:, k % 2, :], part(pb, b, k)).then_inc(pb_full[k % 2], 16)

            @block.gpsimd
            def _(pool):
                pool.sem_inc(y_free, 2)
                with pool.Fori(0, NB) as b:
                    for k in range(NCH):
                        wait_alone(pool, added, b * NCH + k + 1, passed)
                        pool.dma_start(part(x2, b, k), y[:, k % 2, :]).then_inc(y_out, 16)
                        pool.wait_ge(y_out, (b * NCH + k) * 16 + 16)
                        pool.sem_inc(y_free, 1)

            @block.scalar
            def _(act):
                act.sem_inc(evac, 4)
                act.sem_inc(xn_ready, 1)
                with act.Fori(0, NB) as b:
                    act.wait_ge(xn_ready, b * NCH + 1)
                    act.activation(coef[:, :], norm[:, b, :], ACT.Copy).then_inc(coef_ready, 1)
                    act.wait_ge(coef_ready, b + 1)
                    for k in range(NCH + 2):
                        if k < NCH:
                            n = b * NCH + k
                            act.wait_ge(x_full[k % 4], b * (4 * NCH) + 16 * (k // 4 + 1))
                            act.wait_ge(mixed, n + 1)
                            act.activation(xn[:, k % 2, :], x_in[:, k % 4, :], ACT.Identity,
                                           scale=coef[:, 0:1], bias=coef[:, 1:2]).then_inc(xn_ready, 1)
                        if k >= 2:
                            j = k - 2
                            act.wait_ge(mixed, b * NCH + j + 3)
                            act.wait_ge(y_free, b * NCH + j + 1)
                            act.wait_ge(stat, b * NCH + j + 3)
                            act.activation(y[:, j % 2, :], ps[:, j % 4, :, :].rearrange("p k n -> p (k n)"), ACT.Relu,
                                           bias=t["bias1"][:, 0:1]).then_inc(evac, 1)

            @block.vector
            def _(dve):
                dve.wait_ge(gate_full, 32)
                dve.sem_inc(agg_done, 1)
                dve.sem_inc(stat, 4)
                with dve.Fori(0, NB) as b:
                    for k in range(NCH + 2):
                        if k < NCH:
                            n = b * NCH + k
                            dve.wait_ge(xn_ready, n + 2)
                            dve.wait_ge(mixed, n + 1)
                            scan_chunk(dve, n, xn[:, k % 2, :], [gt[:, d, k * LE:(k + 1) * LE] for d in range(2)],
                                       S[:, k % 2, :, :], M[:, k % 2, :, :], step)
                        if k >= 2:
                            j = k - 2
                            m = b * NCH + j
                            dve.wait_ge(evac, m + 5)
                            dve.tensor_tensor(y[:, j % 2, :], y[:, j % 2, :], x_in[:, j % 4, :], ALU.add).then_inc(added, 1)
                            dve.wait_ge(added, m + 1)
                            if j == 0:
                                dve.wait_ge(agg_done, 2 * b + 1)
                            for i in range(2):
                                last = dve.bn_stats(bns[:, 2 * j + i, :], y[:, j % 2, i * 512:(i + 1) * 512])
                            last.then_inc(stat, 1)
                    wait_alone(dve, stat, b * NCH + NCH + 4, passed)
                    dve.bn_aggr(agg[:, :], bns[:, :, :].rearrange("p n s -> p (n s)")).then_inc(agg_done, 1)
                    dve.wait_ge(agg_done, 2 * b + 2)
                    dve.tensor_copy(mv[:, b, :], agg[:, :]).then_inc(agg_done, 1)

            @block.tensor
            def _(pe):
                pe.sem_inc(mixed, 2)
                with pe.Fori(0, NB) as b:
                    for k in range(NCH):
                        n = b * NCH + k
                        pe.wait_ge(step, n * 8 + 8)
                        pe.wait_ge(pb_full[k % 2], b * (8 * NCH) + 16 * (k // 2 + 1))
                        pe.wait_ge(evac, n + 1)
                        mix_directions(nc, ps[:, k % 4, :, :], S[:, k % 2, :, :], M[:, k % 2, :, :],
                                       t["w_dir"], t["w_neg"], 0, (t["ident"][:, :], pb_in[:, k % 2, :])).then_inc(mixed, 1)


DY = 3
CJ = 8
JC = C // CJ
RT = 4
RE = RT * W


def kernels_phase(nc, top, NB, mv, norm, io, kern, mean3):
    with Phase(nc) as mem:
        sb = lambda n, s: mem.enter_context(nc.sbuf_tensor("kn_" + n, s, F32))
        w1, b1 = sb("w1", [P, P]), sb("b1", [P, 1])
        w2, b2, ones = sb("w2", [P, 288]), sb("b2", [1, 288]), sb("ones", [1, NB])
        w2q, b2q = sb("w2q", [P, 12, 3, CJ, Q]), sb("b2q", [1, 12, 3, CJ, Q])
        sel, centre = sb("sel", [P, JC, 96]), sb("centre", [96, 12])
        pooled, hid = sb("pooled", [P, NB]), sb("hid", [P, NB])
        rs3 = sb("rs3", [96, NB, JC])
        ps = mem.enter_context(nc.psum_tensor("kn_ps", [P, 4, 512], F32))
        s = {n: phase_sem(nc, mem, ("kn_" + n)) for n in ("small", "dve", "pooled", "mm", "hid", "wide")}
        with nc.Block() as block:
            @block.sync
            def _(sp):
                loads(sp, s["small"], [
                    (w1[:, :], bass.AP(io["mlp_w1"].tensor, 0, [[P, C], [0, Q], [1, P]])),
                    (b1[:, :], io["mlp_b1"]), (w2[:, :], io["mlp_w2"]), (b2[:, :], io["mlp_b2"]),
                    (sel[:, :, :], io["select_96"].rearrange("p (j m) -> p j m", m=96)), (centre[:, :], io["centre_96"])])

            @block.vector
            def _(dve):
                ch = Chain(dve, s["dve"])
                dve.wait_ge(s["small"], 96)
                dve.memset(ones[:, :], 1.0).then_inc(s["wide"], 1)
                for j in range(JC):
                    for dx in range(3):
                        for src, dst, n in ((w2, w2q, P), (b2, b2q, 1)):
                            v = src[:, 72 * j:72 * j + 72].rearrange("p (c y x) -> p y c x", y=3, x=3)[:, :, :, dx]
                            dve.tensor_copy(dst[:, 3 * j + dx, :, :, :], v.unsqueeze(3).to_broadcast([n, 3, CJ, Q])).then_inc(s["wide"], 1)
                ch.then(dve.tensor_tensor(pooled[:, :], mv[:, :, 0], norm[:, :, 2], ALU.subtract))
                ch.then(dve.scalar_tensor_tensor(pooled[:, :], pooled[:, :], 1.0 / Q, norm[:, :, 0], ALU.mult, ALU.mult))
                dve.sem_inc(s["pooled"], 1)
                dve.wait_ge(s["mm"], 2)
                for j in range(JC):
                    ch.then(dve.tensor_copy(mean3[:, :, j], ps[0:96, 1, j * 64:j * 64 + NB]))
                    ch.then(dve.tensor_copy(rs3[:, :, j], ps[0:96, 2, j * 64:j * 64 + NB]))
                dve.wait_ge(s["mm"], 3)
                raw = ps[0:96, 3, 0:12 * NB].rearrange("p (j x b) -> p b j x", j=JC, x=3)
                for j in range(JC):
                    ch.then(dve.tensor_tensor(kern[:, :, j, :], raw[:, :, j, :],
                                              rs3[:, :, j].unsqueeze(2).to_broadcast([96, NB, 3]), ALU.mult))
                    ch.then(dve.tensor_tensor(kern[:, :, j, :], kern[:, :, j, :],
                                              centre[:, 3 * j:3 * j + 3].unsqueeze(1).to_broadcast([96, NB, 3]), ALU.add))

            @block.tensor
            def _(pe):
                pe.wait_ge(s["small"], 96)
                pe.wait_ge(s["pooled"], 1)
                nc.tensor.matmul(ps[:, 0, 0:NB], w1[:, :], pooled[:, :], start=True, stop=True).then_inc(s["mm"], 1)
                for j in range(JC):
                    nc.tensor.matmul(ps[0:96, 1, j * 64:j * 64 + NB], sel[:, j, :], norm[:, :, 2], start=True, stop=True)
                    last = nc.tensor.matmul(ps[0:96, 2, j * 64:j * 64 + NB], sel[:, j, :], norm[:, :, 0], start=True, stop=True)
                last.then_inc(s["mm"], 1)
                pe.wait_ge(s["hid"], 1)
                pe.wait_ge(s["wide"], 25)
                for n in range(12):
                    out = ps[0:96, 3, n * NB:(n + 1) * NB]
                    nc.tensor.matmul(out, w2q[:, n, :, :, :].rearrange("p y c q -> p (y c q)"), hid[:, :], start=True, stop=False)
                    last = nc.tensor.matmul(out, b2q[:, n, :, :, :].rearrange("p y c q -> p (y c q)"), ones[:, :], start=False, stop=True)
                last.then_inc(s["mm"], 1)

            @block.scalar
            def _(act):
                act.wait_ge(s["mm"], 1)
                act.activation(hid[:, :], ps[:, 0, 0:NB], ACT.Relu, bias=b1[:, 0:1]).then_inc(s["hid"], 1)


def depthwise_phase(nc, top, NB, x2, kern, mean3, io, norm, x3, mv):
    NT = QR // RT
    with Phase(nc) as mem:
        sb = lambda n, s: mem.enter_context(nc.sbuf_tensor("dw_" + n, s, F32))
        tile = sb("tile", [P, 4, JC, RT, W])
        out = sb("out", [P, 2, RE])
        eye = sb("eye", [96, 32])
        inside = sb("inside", [96, 2])
        diag = sb("diag", [P, 2, 12, 32])
        bns, agg = sb("bns", [P, 2 * NT, 6]), sb("agg", [P, 2])
        mean_b, mean_o = sb("mean_b", [96, 2, JC]), sb("mean_o", [P, 2, 1])
        ps = mem.enter_context(nc.psum_tensor("dw_ps", [P, 4, 2, 512], F32))
        sem = lambda n: phase_sem(nc, mem, ("dw_" + n))
        passed = sem("passed")
        small, diag_ready, centred, conved, evac, stat = sem("small"), sem("diag_ready"), sem("centred"), sem("conved"), sem("evac"), sem("stat")
        agg_done, filled, mean_ready, prep = sem("agg"), sem("filled"), sem("mean_ready"), sem("prep")
        t_full, o_out, o_free = [sem(f"t_full{i}") for i in range(4)], sem("o_out"), sem("o_free")
        with nc.Block() as block:
            @block.sync
            def _(sp):
                loads(sp, small, [(eye[:, :], io["eye_96"]), (inside[:, :], io["inside_96"])])
                with sp.Fori(0, NB) as b:
                    for k in range(NT):
                        sp.wait_ge(conved, b * NT + k + 1)
                        for dy in range(DY):
                            src = bass.AP(x2.tensor, (b * C * HW) + W + (k * RT + dy - 1) * W,
                                          [[HW // Q, 32], [CJ * HW, JC], [1, RE]])
                            sp.dma_start(tile[32 * dy:32 * dy + 32, k % 4, :, :, :].rearrange("p j r w -> p j (r w)"), src
                                         ).then_inc(t_full[k % 4], 16)

            @block.gpsimd
            def _(pool):
                pool.sem_inc(o_free, 2)
                with pool.Fori(0, NB) as b:
                    for k in range(NT):
                        wait_alone(pool, evac, b * NT + k + 5, passed)
                        pool.dma_start(x3[b].rearrange("c (q r) w -> (c q) (r w)", q=Q)[:, k * RE:(k + 1) * RE],
                                       out[:, k % 2, :]).then_inc(o_out, 16)
                        pool.wait_ge(o_out, (b * NT + k) * 16 + 16)
                        pool.sem_inc(o_free, 1)

            @block.vector
            def _(dve):
                dve.wait_ge(small, 32)
                dve.sem_inc(stat, 2)
                dve.sem_inc(agg_done, 1)
                dve.memset(tile[96:P, :, :, :, :].rearrange("p s j r w -> p (s j r w)"), 0.0).then_inc(filled, 1)
                dve.memset(diag[96:P, :, :, :].rearrange("p u n m -> p (u n m)"), 0.0).then_inc(filled, 1)
                with dve.Fori(0, NB // 2) as pair:
                    for u in range(2):
                        b = pair * 2 + u
                        dve.wait_ge(conved, b * NT + 4)
                        dve.tensor_tensor(diag[0:96, u, :, :], eye[:, :].unsqueeze(1).to_broadcast([96, 12, 32]),
                                          kern[:, b, :, :].rearrange("p j x -> p (j x)").unsqueeze(2).to_broadcast([96, 12, 32]),
                                          ALU.mult).then_inc(diag_ready, 1)
                        dve.tensor_copy(mean_b[:, u, :], mean3[:, b, :]).then_inc(prep, 1)
                        dve.wait_ge(prep, b + 1)
                        for k in range(NT + 2):
                            if k < NT:
                                n = b * NT + k
                                dve.wait_ge(t_full[k % 4], b * (12 * NT) + 48 * (k // 4 + 1))
                                for j in range(JC):
                                    part = tile[0:96, k % 4, j, :, :].rearrange("p r w -> p (r w)")
                                    last = dve.tensor_scalar(part, part, mean_b[:, u, j:j + 1], None, ALU.subtract)
                                last.then_inc(centred, 1)
                                for edge, dy, row in ((0, 0, 0), (NT - 1, 2, RT - 1)):
                                    if k == edge:
                                        dve.wait_ge(centred, n + 1 + 2 * b + (1 if k else 0))
                                        e = tile[32 * dy:32 * dy + 32, k % 4, :, row, :]
                                        dve.tensor_scalar(e, e, inside[32 * dy:32 * dy + 32, edge > 0:(edge > 0) + 1],
                                                          None, ALU.mult).then_inc(centred, 1)
                            if k >= 2:
                                j = k - 2
                                m = b * NT + j
                                dve.wait_ge(evac, m + 5)
                                if j == 0:
                                    dve.wait_ge(agg_done, 2 * b + 1)
                                for i in range(2):
                                    last = dve.bn_stats(bns[:, 2 * j + i, :], out[:, j % 2, i * 512:(i + 1) * 512])
                                last.then_inc(stat, 1)
                        wait_alone(dve, stat, b * NT + NT + 2, passed)
                        dve.bn_aggr(agg[:, :], bns[:, :, :].rearrange("p n s -> p (n s)")).then_inc(agg_done, 1)
                        dve.wait_ge(agg_done, 2 * b + 2)
                        dve.tensor_copy(mv[:, b, :], agg[:, :]).then_inc(agg_done, 1)

            @block.tensor
            def _(pe):
                pe.sem_inc(conved, 4)
                pe.wait_ge(filled, 2)
                with pe.Fori(0, NB // 2) as pair:
                    for u in range(2):
                        b = pair * 2 + u
                        pe.wait_ge(diag_ready, b + 1)
                        for k in range(NT):
                            n = b * NT + k
                            pe.wait_ge(centred, n + 2 + 2 * b + (1 if k == NT - 1 else 0))
                            pe.wait_ge(evac, n + 1)
                            for h in range(2):
                                for i, dx in enumerate((1, 0, 2)):
                                    w0, w1 = max(0, 1 - dx), min(W, W + 1 - dx)
                                    for j in range(JC):
                                        o = ps[32 * j:32 * j + 32, k % 4, h, :].rearrange("p (r w) -> p r w", w=W)
                                        last = nc.tensor.matmul(o[:, :, w0:w1], diag[:, u, 3 * j + dx, :],
                                                                tile[:, k % 4, j, 2 * h:2 * h + 2, w0 + dx - 1:w1 + dx - 1],
                                                                start=(i == 0), stop=(i == 2), tile_position=(0, 32 * j))
                            last.then_inc(conved, 1)

            @block.scalar
            def _(act):
                act.sem_inc(evac, 4)
                with act.Fori(0, NB // 2) as pair:
                    for u in range(2):
                        b = pair * 2 + u
                        act.wait_ge(evac, b * NT + 4)
                        act.activation(mean_o[:, u, :], norm[:, b, 2:3], ACT.Copy).then_inc(mean_ready, 1)
                        act.wait_ge(mean_ready, b + 1)
                        for k in range(NT):
                            act.wait_ge(conved, b * NT + k + 5)
                            act.wait_ge(o_free, b * NT + k + 1)
                            act.wait_ge(stat, b * NT + k + 1)
                            act.activation(out[:, k % 2, :], ps[:, k % 4, :, :].rearrange("p k n -> p (k n)"), ACT.Identity,
                                           bias=mean_o[:, u, :]).then_inc(evac, 1)


def gate_phase(nc, top, NB, x3, io, t, norm, fs, maps):
    NT = QR // RT
    with Phase(nc) as mem:
        sb = lambda n, s: mem.enter_context(nc.sbuf_tensor("ga_" + n, s, F32))
        x_in, xn, prod, f = sb("x_in", [P, 4, RE]), sb("xn", [P, 4, RE]), sb("prod", [P, 2, RE]), sb("f", [P, 4, RE])
        rmax, rsum = sb("rmax", [P, 2, RT // 2, W]), sb("rsum", [P, 2, RT // 2, W])
        pmax, psumm, gate = sb("pmax", [P, 2, RE // 4]), sb("psum", [P, 2, RE // 4]), sb("gate", [P, 2, RE // 4])
        coef = sb("coef", [P, 3])
        ca = sb("ca", [Q, 2, RE])
        cmT = sb("cmT", [P, 2, Q, QR])
        cm = sb("cm", [P, 2, 2, P])
        psF = mem.enter_context(nc.psum_tensor("ga_psF", [P, 2, 512], F32))
        psT = mem.enter_context(nc.psum_tensor("ga_psT", [P, 2, RT, P], F32))
        psC = mem.enter_context(nc.psum_tensor("ga_psC", [Q, 2, 512], F32))
        psM = mem.enter_context(nc.psum_tensor("ga_psM", [P, 2, 2, P], F32))
        sem = lambda n: phase_sem(nc, mem, ("ga_" + n))
        passed = sem("passed")
        x_full = [sem(f"x_full{i}") for i in range(4)]
        f_out, ca_out, f_free, ca_free, cm_free = sem("f_out"), sem("ca_out"), sem("f_free"), sem("ca_free"), sem("cm_free")
        coef_ready, xn_ready, pool_step, sig, gated = sem("coef_ready"), sem("xn_ready"), sem("pool_step"), sem("sig"), sem("gated")
        conved, f_ready, turned, maxed, ca_ready, cm_turned, cm_ready, cm_out = (sem("conved"), sem("f_ready"), sem("turned"), sem("maxed"),
                                                                               sem("ca_ready"), sem("cm_turned"), sem("cm_ready"), sem("cm_out"))
        part = lambda a, b, k: a[b].rearrange("c (q r) w -> (c q) (r w)", q=Q)[:, k * RE:(k + 1) * RE]
        plane = MAPW * 2 * MAPW
        with nc.Block() as block:
            @block.sync
            def _(sp):
                with sp.Fori(0, NB) as b:
                    for k in range(NT):
                        sp.wait_ge(xn_ready, b * NT + k + 1)
                        sp.dma_start(x_in[:, k % 4, :], part(x3, b, k)).then_inc(x_full[k % 4], 16)

            @block.gpsimd
            def _(pool):
                pool.sem_inc(f_free, 4)
                pool.sem_inc(ca_free, 2)
                pool.sem_inc(cm_free, 1)
                with pool.Fori(0, NB) as b:
                    for k in range(NT):
                        n = b * NT + k
                        wait_alone(pool, f_ready, n + 2, passed)
                        pool.dma_start(part(fs, b, k), f[:, k % 4, :]).then_inc(f_out, 16)
                        wait_alone(pool, ca_ready, n + 3, passed)
                        pool.dma_start(bass.AP(maps.tensor, b * plane + (PAD + k * RT) * 2 * MAPW + MAPW + PAD,
                                               [[QR * 2 * MAPW, Q], [2 * MAPW, RT], [1, W]]),
                                       ca[:, k % 2, :].rearrange("p (r w) -> p r w", w=W)).then_inc(ca_out, 16)
                        pool.wait_ge(f_out, n * 16 + 16)
                        pool.sem_inc(f_free, 1)
                        pool.wait_ge(ca_out, n * 16 + 16)
                        pool.sem_inc(ca_free, 1)
                    wait_alone(pool, cm_ready, b + 2, passed)
                    for h in range(2):
                        pool.dma_start(bass.AP(maps.tensor, b * plane + (PAD + h * P) * 2 * MAPW + PAD, [[2 * MAPW, P], [1, W]]),
                                       cm[:, h, :, :].rearrange("p a w -> p (a w)")).then_inc(cm_out, 16)
                    pool.wait_ge(cm_out, b * 32 + 32)
                    pool.sem_inc(cm_free, 1)

            @block.scalar
            def _(act):
                act.sem_inc(xn_ready, 4)
                act.sem_inc(ca_ready, 2)
                act.sem_inc(f_ready, 1)
                act.sem_inc(cm_ready, 1)
                act.sem_inc(sig, 2)
                with act.Fori(0, NB) as b:
                    act.wait_ge(xn_ready, b * NT + 4)
                    act.activation(coef[:, :], norm[:, b, :], ACT.Copy).then_inc(coef_ready, 1)
                    act.wait_ge(coef_ready, b + 1)
                    for k in range(-1, NT + 3):
                        if k + 1 < NT:
                            n = b * NT + k + 1
                            act.wait_ge(x_full[(k + 1) % 4], b * (4 * NT) + 16 * ((k + 1) // 4 + 1))
                            act.wait_ge(conved, n + 1)
                            act.activation(xn[:, (k + 1) % 4, :], x_in[:, (k + 1) % 4, :], ACT.Identity,
                                           scale=coef[:, 0:1], bias=coef[:, 1:2]).then_inc(xn_ready, 1)
                        if 0 <= k < NT:
                            m = b * NT + k
                            act.wait_ge(pool_step, 5 * m + 5)
                            act.wait_ge(gated, m + 1)
                            act.activation(gate[:, k % 2, :], psumm[:, k % 2, :], ACT.Sigmoid,
                                           scale=t["mlp"][:, 0:1], bias=t["mlp"][:, 1:2]).then_inc(sig, 1)
                        if k >= 3:
                            j = k - 3
                            m = b * NT + j
                            act.wait_ge(turned, m + 2)
                            act.wait_ge(ca_free, m + 1)
                            act.activation(ca[:, j % 2, :], psC[:, :, :].rearrange("p k n -> p (k n)"), ACT.Copy).then_inc(ca_ready, 1)
                        if 2 <= k < NT + 2:
                            j = k - 2
                            m = b * NT + j
                            act.wait_ge(conved, m + 5)
                            act.wait_ge(f_free, m + 1)
                            act.wait_ge(turned, m + 1)
                            act.activation(f[:, j % 4, :], psF[:, :, :].rearrange("p k n -> p (k n)"), ACT.Identity,
                                           bias=t["bias3"][:, 0:1]).then_inc(f_ready, 1)
                    act.wait_ge(cm_turned, b + 2)
                    act.wait_ge(cm_free, b + 1)
                    act.activation(cm[:, :, :, :], psM[:, :, :, :], ACT.Copy).then_inc(cm_ready, 1)

            @block.vector
            def _(dve):
                dve.sem_inc(gated, 2)
                dve.sem_inc(maxed, 1)
                with dve.Fori(0, NB) as b:
                    for k in range(NT + 3):
                        if k < NT:
                            n = b * NT + k
                            s = k % 2
                            rows = xn[:, k % 4, :].rearrange("p (r e w) -> p r e w", e=2, w=W)
                            dve.wait_ge(xn_ready, n + 5)
                            dve.wait_ge(sig, n + 1)
                            dve.tensor_tensor(rmax[:, s, :, :], rows[:, :, 0, :], rows[:, :, 1, :], ALU.max).then_inc(pool_step, 1)
                            dve.tensor_tensor(rsum[:, s, :, :], rows[:, :, 0, :], rows[:, :, 1, :], ALU.add).then_inc(pool_step, 1)
                            dve.wait_ge(pool_step, 5 * n + 1)
                            cols = rmax[:, s, :, :].rearrange("p r (w e) -> p (r w) e", e=2)
                            dve.tensor_tensor(pmax[:, s, :], cols[:, :, 0], cols[:, :, 1], ALU.max).then_inc(pool_step, 1)
                            dve.wait_ge(pool_step, 5 * n + 2)
                            cols = rsum[:, s, :, :].rearrange("p r (w e) -> p (r w) e", e=2)
                            dve.tensor_tensor(psumm[:, s, :], cols[:, :, 0], cols[:, :, 1], ALU.add).then_inc(pool_step, 1)
                            dve.wait_ge(pool_step, 5 * n + 4)
                            dve.scalar_tensor_tensor(psumm[:, s, :], psumm[:, s, :], 0.25, pmax[:, s, :], ALU.mult, ALU.add).then_inc(pool_step, 1)
                        if 1 <= k <= NT:
                            m = b * NT + k - 1
                            s = (k - 1) % 2
                            dve.wait_ge(sig, m + 3)
                            dve.wait_ge(conved, m + 3)
                            for e in range(2):
                                src = xn[:, (k - 1) % 4, :].rearrange("p (r e w) -> p r e w", e=2, w=W)[:, :, e, :]
                                dst = prod[:, s, :].rearrange("p (r e w) -> p r e w", e=2, w=W)[:, :, e, :]
                                g = gate[:, s, :].rearrange("p (r w) -> p r w", r=RT // 2).unsqueeze(3).to_broadcast([P, RT // 2, W // 2, 2])
                                last = dve.tensor_tensor(dst.rearrange("p r (w f) -> p r w f", f=2), src.rearrange("p r (w f) -> p r w f", f=2), g, ALU.mult)
                            last.then_inc(gated, 1)
                        if k >= 3:
                            j = k - 3
                            dve.wait_ge(turned, b * NT + j + 2)
                            if j == 0:
                                dve.wait_ge(cm_turned, b + 1)
                            for h in range(2):
                                last = dve.tensor_reduce(cmT[:, h, :, j * RT:(j + 1) * RT].rearrange("p q r -> p r q"),
                                                         psT[:, h, :, :].rearrange("p r (o q) -> p r q o", q=Q), AX.X, ALU.max)
                            last.then_inc(maxed, 1)

            @block.tensor
            def _(pe):
                pe.sem_inc(conved, 4)
                pe.sem_inc(turned, 1)
                pe.sem_inc(cm_turned, 1)
                with pe.Fori(0, NB) as b:
                    for k in range(NT + 1):
                        if k < NT:
                            n = b * NT + k
                            pe.wait_ge(gated, n + 3)
                            pe.wait_ge(f_ready, n + 1)
                            for h in range(2):
                                nc.tensor.matmul(psF[:, h, :], t["w_mix"][:, 1, :], xn[:, k % 4, h * 512:(h + 1) * 512], start=True, stop=False)
                                last = nc.tensor.matmul(psF[:, h, :], t["w_mix"][:, 0, :], prod[:, k % 2, h * 512:(h + 1) * 512], start=False, stop=True)
                            last.then_inc(conved, 1)
                        if k >= 1:
                            j = k - 1
                            m = b * NT + j
                            pe.wait_ge(f_ready, m + 2)
                            pe.wait_ge(maxed, m + 1)
                            pe.wait_ge(ca_ready, m + 2)
                            for h in range(2):
                                for r in range(RT):
                                    nc.tensor.transpose(psT[:, h, r, :], f[:, j % 4, r * W + h * P:r * W + (h + 1) * P], t["ident"][:, :])
                            for h in range(2):
                                last = nc.tensor.matmul(psC[:, h, :], t["chan_mean"][:, :], f[:, j % 4, h * 512:(h + 1) * 512], start=True, stop=True)
                            last.then_inc(turned, 1)
                    pe.wait_ge(maxed, b * NT + NT + 1)
                    pe.wait_ge(cm_ready, b + 1)
                    for a in range(2):
                        for h in range(2):
                            last = nc.tensor.transpose(psM[:, a, h, :], cmT[:, h, 2 * a:2 * a + 2, :].rearrange("p q r -> p (q r)"), t["ident"][:, :])
                    last.then_inc(cm_turned, 1)


def attention_phase(nc, top, NB, x3, io, t, fs, maps, y):
    RA = 8
    AE = RA * W
    NT = QR // RA
    MW = MAPW - 2
    with Phase(nc) as mem:
        sb = lambda n, s: mem.enter_context(nc.sbuf_tensor("at_" + n, s, F32))
        rows = sb("rows", [P, 4, RA, MW])
        x_in, f_in, a = sb("x_in", [P, 4, AE]), sb("f_in", [P, 4, AE]), sb("a", [P, 2, AE])
        w = sb("w", [P, 4, P])
        wa, quarter = sb("wa", [P, 4, C]), sb("quarter", [P, Q])
        ps = mem.enter_context(nc.psum_tensor("at_ps", [P, 2, 4, 512], F32))
        sem = lambda n: phase_sem(nc, mem, ("at_" + n))
        passed = sem("passed")
        zeroed, small, widened, conved, sig, scaled, done = sem("zeroed"), sem("small"), sem("widened"), sem("conved"), sem("sig"), sem("scaled"), sem("done")
        r_full, xf_full = [sem(f"r_full{i}") for i in range(4)], [sem(f"xf_full{i}") for i in range(4)]
        y_out, y_free = sem("y_out"), sem("y_free")
        plane = MAPW * 2 * MAPW
        part = lambda v, b, k: v[b].rearrange("c (q r) w -> (c q) (r w)", q=Q)[:, k * AE:(k + 1) * AE]
        with nc.Block() as block:
            @block.sync
            def _(sp):
                sp.wait_ge(zeroed, 1)
                n = 1
                sp.dma_start(quarter[:, :], io["quarter_att"]).then_inc(small, 16)
                for q in range(Q):
                    for p in range(4):
                        for s in range(2):
                            if 2 * p + s < 7:
                                sp.dma_start(wa[32 * q + s:32 * q + s + 27:2, p, :], io["att_w"][2 * p + s]).then_inc(small, 16)
                                n += 1
                sp.wait_ge(small, 16 * n)
                with sp.Fori(0, NB) as b:
                    for k in range(NT):
                        sp.wait_ge(conved, b * NT + k + 1)
                        for q in range(Q):
                            for s in range(2):
                                sp.dma_start(rows[32 * q + s:32 * q + s + 31:2, k % 4, :, :],
                                             bass.AP(maps.tensor, b * plane + (QR * q + k * RA) * 2 * MAPW + s,
                                                     [[MAPW, 16], [2 * MAPW, RA], [1, MW]])).then_inc(r_full[k % 4], 16)
                        sp.wait_ge(y_free, b * NT + k + 1)
                        sp.dma_start(x_in[:, k % 4, :], part(x3, b, k)).then_inc(xf_full[k % 4], 16)
                        sp.dma_start(f_in[:, k % 4, :], part(fs, b, k)).then_inc(xf_full[k % 4], 16)

            @block.gpsimd
            def _(pool):
                pool.sem_inc(y_free, 4)
                with pool.Fori(0, NB) as b:
                    for k in range(NT):
                        wait_alone(pool, done, b * NT + k + 1, passed)
                        pool.dma_start(part(y, b, k), x_in[:, k % 4, :]).then_inc(y_out, 16)
                        pool.wait_ge(y_out, (b * NT + k) * 16 + 16)
                        pool.sem_inc(y_free, 1)

            @block.tensor
            def _(pe):
                pe.wait_ge(widened, 4)
                pe.sem_inc(conved, 4)
                with pe.Fori(0, NB) as b:
                    for k in range(NT):
                        pe.wait_ge(r_full[k % 4], b * (32 * NT) + 128 * (k // 4 + 1))
                        pe.wait_ge(sig, b * NT + k + 1)
                        for h in range(4):
                            for p in range(4):
                                last = nc.tensor.matmul(ps[:, k % 2, h, :].rearrange("p (r w) -> p r w", w=W), w[:, p, :],
                                                        rows[:, k % 4, 2 * h:2 * h + 2, 2 * p:2 * p + W], start=(p == 0), stop=(p == 3))
                        last.then_inc(conved, 1)

            @block.scalar
            def _(act):
                act.sem_inc(sig, 2)
                with act.Fori(0, NB) as b:
                    for k in range(NT):
                        act.wait_ge(conved, b * NT + k + 5)
                        act.wait_ge(scaled, b * NT + k + 1)
                        act.activation(a[:, k % 2, :], ps[:, k % 2, :, :].rearrange("p h n -> p (h n)"), ACT.Sigmoid,
                                       bias=t["bias_att"][:, 0:1]).then_inc(sig, 1)

            @block.vector
            def _(dve):
                dve.memset(wa[:, :, :], 0.0).then_inc(zeroed, 1)
                dve.wait_ge(small, 16 * 29)
                for p in range(4):
                    dve.tensor_tensor(w[:, p, :].rearrange("p (o q) -> p o q", q=Q), wa[:, p, :].unsqueeze(2).to_broadcast([P, C, Q]),
                                      quarter[:, :].unsqueeze(1).to_broadcast([P, C, Q]), ALU.mult).then_inc(widened, 1)
                dve.sem_inc(scaled, 2)
                with dve.Fori(0, NB) as b:
                    for k in range(NT):
                        n = b * NT + k
                        dve.wait_ge(sig, n + 3)
                        dve.wait_ge(xf_full[k % 4], b * (8 * NT) + 32 * (k // 4 + 1))
                        dve.tensor_tensor(f_in[:, k % 4, :], a[:, k % 2, :], f_in[:, k % 4, :], ALU.mult).then_inc(scaled, 1)
                        dve.wait_ge(scaled, n + 3)
                        dve.tensor_tensor(x_in[:, k % 4, :], x_in[:, k % 4, :], f_in[:, k % 4, :], ALU.add).then_inc(done, 1)


def program(nc, NB, io, y, upto=9):
    dram = lambda n, s: nc.dram_tensor(n, s, F32, kind="Internal").ap()
    gates = dram("gates", (4, H, W))
    maps = dram("maps", (NB, MAPW, 2, MAPW))
    Y = dram("modes", (NB, 2, C, M1, M2))
    x1, pb = dram("x1", (NB, C, H, W)), dram("pb", (NB, C, H, W))
    x2_all = dram("x2", (NB * C * HW + 2 * W,))
    x2 = x2_all[W:W + NB * C * HW].rearrange("(b c h w) -> b c h w", c=C, h=H, w=W)
    x3, fs = dram("x3", (NB, C, H, W)), dram("fs", (NB, C, H, W))
    with ExitStack() as top:
        keep = lambda n, s: top.enter_context(nc.sbuf_tensor("keep_" + n, s, F32))
        t = {"w_dir": keep("w_dir", [P, 4, P]), "w_neg": keep("w_neg", [P, 4, P]), "w_mix": keep("w_mix", [P, 2, P]),
             "ident": keep("ident", [P, P]), "group_avg": keep("group_avg", [P, P]),
             "mask_cq": keep("mask_cq", [P, G]), "mask_jc": keep("mask_jc", [P, G]), "chan_mean": keep("chan_mean", [P, Q]), "quarter": keep("quarter", [P, Q]),
             "bias1": keep("bias1", [P, 1]), "bias3": keep("bias3", [P, 1]), "bias_att": keep("bias_att", [P, 1]),
             "mlp": keep("mlp", [P, 2])}
        norm = keep("norm", [P, NB, 3])
        mv = keep("mv", [P, NB, 2])
        guard = bass.AP(x2_all.tensor, 0, [[NB * C * HW + W, 2], [1, W]])
        setup_phase(nc, top, io, gates, maps, guard, t)
        with ExitStack() as spectral:
            bn = spectral.enter_context(nc.sbuf_tensor("bn", [P, NB, C, 6], F32))
            with ExitStack() as modes:
                X = modes.enter_context(nc.sbuf_tensor("X", [P, NB, NG * 64], F32))
                spectrum_phase(nc, top, NB, io["x"], io, bn, X)
                stats_from_rows(nc, top, "st0_", NB, bn[:, :, :, :], t["mask_jc"][:, :], norm)
                mixing_phase(nc, top, NB, io, X, norm, Y)
            if upto < 1:
                return
            inverse_phase(nc, top, NB, io["x"], io, Y, x1, bn)
            stats_from_rows(nc, top, "st1_", NB, bn[:, :, :, :], t["mask_cq"][:, :], norm)
        if upto < 2:
            return
        vertical_phase(nc, top, NB, x1, gates, t, norm, pb)
        if upto < 3:
            return
        horizontal_phase(nc, top, NB, x1, pb, gates, t, norm, x2, mv)
        stats_from_quarters(nc, top, "st2_", NB, mv, t, norm)
        if upto < 4:
            return
        with ExitStack() as dyn:
            kern = dyn.enter_context(nc.sbuf_tensor("kern", [96, NB, JC, 3], F32))
            mean3 = dyn.enter_context(nc.sbuf_tensor("mean3", [96, NB, JC], F32))
            kernels_phase(nc, top, NB, mv, norm, io, kern, mean3)
            depthwise_phase(nc, top, NB, x2, kern, mean3, io, norm, x3, mv)
        stats_from_quarters(nc, top, "st3_", NB, mv, t, norm)
        if upto < 5:
            return
        gate_phase(nc, top, NB, x3, io, t, norm, fs, maps)
        if upto < 6:
            return
        attention_phase(nc, top, NB, x3, io, t, fs, maps, y)


def constants():
    k, n = np.arange(M1), np.arange(H)
    ang = 2 * np.pi * ((n[:, None] * k[None, :]) % H) / H
    cos, sin = np.cos(ang), np.sin(ang)
    weight = np.where(k == 0, 1.0, 2.0) / HW
    inv_w = np.concatenate([weight[:, None] * cos.T, -weight[:, None] * sin.T])
    p = np.arange(P)
    c_of, q_of = p // Q, p % Q
    r96 = np.arange(96)
    dy, c8, q3 = r96 // 32, (r96 % 32) // Q, r96 % Q
    sel = np.zeros((P, JC, 96))
    for j in range(JC):
        sel[:, j] = (c_of[:, None] == CJ * j + c8[None, :]) & (q_of[:, None] == q3[None, :])
    centre = np.zeros((96, JC, 3))
    centre[dy == 1, :, 1] = 1.0
    inside = np.ones((96, 2))
    inside[(dy == 0) & (q3 == 0), 0] = 0.0
    inside[(dy == 2) & (q3 == Q - 1), 1] = 0.0
    out = {
        "dft_h": np.concatenate([cos, sin], 1),
        "dft_w": np.stack([np.concatenate([cos, -sin], 1), np.concatenate([-sin, -cos], 1)], 1),
        "idft_h": np.concatenate([cos.T, sin.T]),
        "idft_w": np.kron(np.eye(2), inv_w),
        "ident": np.eye(P),
        "group_avg": (c_of[:, None] // 2 == c_of[None, :] // 2) / (2.0 * Q),
        "mask_cq": (c_of[:, None] // 2 == np.arange(G)[None, :]),
        "mask_jc": ((p % C)[:, None] // 2 == np.arange(G)[None, :]),
        "chan_mean": (q_of[:, None] == np.arange(Q)[None, :]) / float(C),
        "quarter": q_of[:, None] == np.arange(Q)[None, :],
        "quarter_att": (p // C)[:, None] == np.arange(Q)[None, :],
        "select_96": sel.reshape(P, JC * 96),
        "centre_96": centre.reshape(96, 12),
        "inside_96": inside,
        "eye_96": np.concatenate([np.eye(32)] * 3),
    }
    return {n: np.ascontiguousarray(v, np.float32) for n, v in out.items()}


def layouts(x, L0_conv_coeff_real, L0_conv_coeff_imag, L0_conv_proj, L1_conv_weights, L1_conv_conv_w, L1_conv_conv_b,
            L2_conv_w1, L2_conv_b1, L2_conv_w2, L2_conv_b2, L3_conv_mlp_w, L3_conv_mlp_b, L3_conv_conv_w, L3_conv_conv_b,
            L3_conv_convout_w, L3_conv_convout_b):
    a = np.asarray
    up, down, left, right = a(L1_conv_weights)
    modes_last = lambda v: a(v).reshape(C, C, NG, J, M2).transpose(0, 2, 4, 3, 1)
    out = {
        "x": a(x), "coeff_real": modes_last(L0_conv_coeff_real), "coeff_imag": modes_last(L0_conv_coeff_imag), "proj_T": a(L0_conv_proj).T,
        "scan_w": np.stack([left, right, up.T, down.T]),
        "conv1_T": a(L1_conv_conv_w).T, "conv1_b": a(L1_conv_conv_b),
        "mlp_w1": a(L2_conv_w1), "mlp_b1": a(L2_conv_b1).reshape(P, 1), "mlp_w2": a(L2_conv_w2), "mlp_b2": a(L2_conv_b2).reshape(1, -1),
        "mlp_w": a(L3_conv_mlp_w).reshape(1), "mlp_b": a(L3_conv_mlp_b).reshape(1),
        "conv3_T": a(L3_conv_conv_w).reshape(C, 2 * C).T, "conv3_b": a(L3_conv_conv_b),
        "att_w": a(L3_conv_convout_w).transpose(3, 2, 1, 0).reshape(7, 14, C), "att_b": a(L3_conv_convout_b),
    }
    return {n: np.ascontiguousarray(v) for n, v in out.items()}


def kernel(**inputs):
    import concourse.bacc as bacc
    from concourse.bass_utils import run_bass_kernel_spmd

    nc = bacc.Bacc("TRN2", target_bir_lowering=False, num_devices=1)
    arrays = {**layouts(**inputs), **constants()}
    io = {n: nc.dram_tensor(n, v.shape, mybir.dt.from_np(v.dtype), kind="ExternalInput").ap() for n, v in arrays.items()}
    NB = arrays["x"].shape[0]
    y = nc.dram_tensor("y", (NB, C, H, W), F32, kind="ExternalOutput").ap()
    program(nc, NB, io, y)
    r = run_bass_kernel_spmd(nc, [arrays], core_ids=[0])
    return r.results[0]["y"]
```

```python
from contextlib import ExitStack

import numpy as np

import concourse.bass as bass
from concourse import mybir

F32 = mybir.dt.float32
ALU = mybir.AluOpType
ACT = mybir.ActivationFunctionType
AX = mybir.AxisListType

P = 128
C = 32
H = W = 256
Q = P // C
QR = H // Q
HW = H * W
G = 16
M1 = M2 = 32
J = 4
NG = M1 // J
EPS = 1e-5
MAPW = 264
PAD = 3


class Chain:

    def __init__(self, eng, sem, base=0):
        self.eng, self.sem, self.base, self.n = eng, sem, base, 0

    def then(self, ins):
        self.n += 1
        ins.then_inc(self.sem, 1)
        self.eng.wait_ge(self.sem, self.base + self.n)


def phase_sem(nc, mem, name):
    handle = nc.alloc_semaphore(name=name)
    mem.sems.append(handle)
    return handle


def wait_alone(eng, sem, value, passed):
    eng.wait_ge(sem, value)
    eng.sem_inc(passed, 1)


class Phase(ExitStack):

    def __init__(self, nc):
        super().__init__()
        self.nc, self.sems = nc, []

    def __exit__(self, *exc):
        if exc[0] is None:
            self.nc.clear_and_free_semaphores(self.sems)
            self.nc.all_engine_barrier()
        return super().__exit__(*exc)


def loads(eng, sem, pairs):
    for dst, src in pairs:
        eng.dma_start(dst, src).then_inc(sem, 16)
    eng.wait_ge(sem, 16 * len(pairs))


def rstd_of(nc, eng, chain, act_sem, back_sem, var, out, tmp):
    chain.then(eng.tensor_scalar(var, var, EPS, None, ALU.add))
    eng.sem_inc(act_sem, 1)
    eng.wait_ge(back_sem, 1)
    chain.then(eng.reciprocal(out, tmp))
    chain.then(eng.tensor_tensor(tmp, out, out, ALU.mult))
    chain.then(eng.tensor_tensor(tmp, tmp, var, ALU.mult))
    chain.then(eng.tensor_scalar(tmp, tmp, -0.5, 1.5, ALU.mult, ALU.add))
    chain.then(eng.tensor_tensor(out, out, tmp, ALU.mult))


def setup_phase(nc, top, io, gates, x2_guard, t):
    with Phase(nc) as mem:
        sb = lambda n, s: mem.enter_context(nc.sbuf_tensor(n, s, F32))
        raw = sb("gate_raw", [P, 4, 2, H])
        sig = sb("gate_sig", [P, 4, 2, H])
        zero = sb("zero_rows", [2, W])
        wd, wm = sb("wd", [P, 4, C]), sb("wm", [P, 2, C])
        s = {n: phase_sem(nc, mem, ("set_" + n)) for n in
             ("raw", "small", "zeroed", "wide", "sig", "out", "neg")}
        with nc.Block() as block:
            @block.sync
            def _(sp):
                sp.dma_start(raw[:, :, :, :], io["scan_w"].rearrange("d (p l) k -> p d l k", p=P)).then_inc(s["raw"], 16)
                n = 6
                for dst, src, m in ((wd, "conv1_T", 4), (wm, "conv3_T", 2)):
                    for i in range(m):
                        sp.dma_start(dst[:, i, :], bass.AP(io[src].tensor, i * C * C, [[C, C], [0, Q], [1, C]])).then_inc(s["small"], 16)
                for name, src in (("bias1", "conv1_b"), ("bias3", "conv3_b"), ("bias_att", "att_b")):
                    sp.dma_start(t[name][:, :], bass.AP(io[src].tensor, 0, [[1, C], [0, Q], [1, 1]])).then_inc(s["small"], 16)
                    n += 1
                for k, name in enumerate(("mlp_w", "mlp_b")):
                    sp.dma_start(t["mlp"][:, k:k + 1], bass.AP(io[name].tensor, 0, [[0, P], [1, 1]])).then_inc(s["small"], 16)
                    n += 1
                for name in ("ident", "group_avg", "mask_cq", "mask_jc", "chan_mean", "quarter"):
                    sp.dma_start(t[name][:, :], io[name]).then_inc(s["small"], 16)
                    n += 1
                sp.wait_ge(s["small"], 16 * n)
                sp.wait_ge(s["zeroed"], 1)
                sp.wait_ge(s["sig"], 1)
                sp.dma_start(gates.rearrange("d (p l) k -> p d l k", p=P), sig[:, :, :, :]).then_inc(s["out"], 16)
                sp.dma_start(x2_guard, zero[0:2, 0:W]).then_inc(s["out"], 16)
                n_out = 2
                sp.wait_ge(s["out"], 16 * n_out)

            @block.vector
            def _(dve):
                dve.memset(zero[:, :], 0.0).then_inc(s["zeroed"], 1)
                dve.memset(sig[:, :, :, :], 0.0).then_inc(s["zeroed"], 1)
                dve.wait_ge(s["small"], 16 * 17)
                for k, (dst, src, m) in enumerate(((t["w_dir"], wd, 4), (t["w_mix"], wm, 2))):
                    for i in range(m):
                        dve.tensor_tensor(dst[:, i, :].rearrange("p (o q) -> p o q", q=Q),
                                          src[:, i, :].unsqueeze(2).to_broadcast([P, C, Q]),
                                          t["quarter"][:, :].unsqueeze(1).to_broadcast([P, C, Q]), ALU.mult).then_inc(s["wide"], 1)
                dve.wait_ge(s["wide"], 6)
                dve.tensor_scalar(t["w_neg"][:, :, :], t["w_dir"][:, :, :], -1.0, None, ALU.mult).then_inc(s["neg"], 1)
                dve.tensor_scalar(t["mlp"][:, 1:2], t["mlp"][:, 1:2], 2.0, None, ALU.mult).then_inc(s["neg"], 1)

            @block.scalar
            def _(act):
                act.wait_ge(s["raw"], 16)
                act.wait_ge(s["zeroed"], 2)
                for i in range(4):
                    fwd = i % 2 == 0
                    dst = sig[:, i, :, 1:H] if fwd else sig[:, i, :, 0:H - 1]
                    src = raw[:, i, :, 0:H - 1] if fwd else raw[:, i, :, 1:H]
                    last = act.activation(dst, src, ACT.Sigmoid)
                last.then_inc(s["sig"], 1)


def stats_from_rows(nc, top, tag, NB, bn, mask, norm):
    E = NB * C * 2
    with Phase(nc) as mem:
        sb = lambda n, s: mem.enter_context(nc.sbuf_tensor(tag + n, s, F32))
        ones = sb("ones", [P, P])
        dev = sb("dev", [P, E])
        mg, vg, rg, tg = (sb(n, [P, NB * G]) for n in ("mg", "vg", "rg", "tg"))
        spread = sb("spread", [P, 2, NB, G])
        ps = mem.enter_context(nc.psum_tensor(tag + "ps", [P, E], F32))
        s = {n: phase_sem(nc, mem, (tag + n)) for n in ("dve", "mm", "feed", "root", "rooted")}
        entry = bn.rearrange("p b c (e s) -> p (b c e) s", s=3)
        mean_i, m2_i = entry[:, :, 1], entry[:, :, 2]
        with nc.Block() as block:
            @block.vector
            def _(dve):
                ch = Chain(dve, s["dve"])
                ch.then(dve.memset(ones[:, :], 1.0 / (P * 4)))
                dve.sem_inc(s["feed"], 1)
                dve.wait_ge(s["mm"], 1)
                ch.then(dve.tensor_reduce(mg[:, :], ps[:, :].rearrange("p (g e) -> p g e", e=4), AX.X, ALU.add))
                ch.then(dve.tensor_tensor(dev[:, :].rearrange("p (g e) -> p g e", e=4),
                                          mean_i.rearrange("p (g e) -> p g e", e=4),
                                          mg[:, :].unsqueeze(2).to_broadcast([P, NB * G, 4]), ALU.subtract))
                ch.then(dve.tensor_tensor(dev[:, :], dev[:, :], dev[:, :], ALU.mult))
                ch.then(dve.scalar_tensor_tensor(dev[:, :], m2_i, 1.0 / W, dev[:, :], ALU.mult, ALU.add))
                dve.sem_inc(s["feed"], 1)
                dve.wait_ge(s["mm"], 2)
                ch.then(dve.tensor_reduce(vg[:, :], ps[:, :].rearrange("p (g e) -> p g e", e=4), AX.X, ALU.add))
                rstd_of(nc, dve, ch, s["root"], s["rooted"], vg[:, :], rg[:, :], tg[:, :])
                for k, v in enumerate((rg, mg)):
                    ch.then(dve.tensor_tensor(spread[:, k, :, :], v[:, :].rearrange("p (b g) -> p b g", g=G),
                                              mask.unsqueeze(1).to_broadcast([P, NB, G]), ALU.mult))
                ch.then(dve.tensor_reduce(norm[:, :, 0], spread[:, 0, :, :], AX.X, ALU.add))
                ch.then(dve.tensor_reduce(norm[:, :, 2], spread[:, 1, :, :], AX.X, ALU.add))
                ch.then(dve.scalar_tensor_tensor(norm[:, :, 1], norm[:, :, 0], -1.0, norm[:, :, 2], ALU.mult, ALU.mult))

            @block.tensor
            def _(pe):
                for k in range(2):
                    pe.wait_ge(s["feed"], k + 1)
                    src = mean_i if k == 0 else dev[:, :]
                    for n in range(0, E, 512):
                        m = min(512, E - n)
                        last = nc.tensor.matmul(ps[:, n:n + m], ones[:, :], src[:, n:n + m], start=True, stop=True)
                    last.then_inc(s["mm"], 1)

            @block.scalar
            def _(act):
                act.wait_ge(s["root"], 1)
                act.activation(tg[:, :], vg[:, :], ACT.Sqrt).then_inc(s["rooted"], 1)


def stats_from_quarters(nc, top, tag, NB, mv, t, norm):
    with Phase(nc) as mem:
        sb = lambda n, s: mem.enter_context(nc.sbuf_tensor(tag + n, s, F32))
        dev = sb("dev", [P, NB])
        var, rs, tmp = sb("var", [P, NB]), sb("rs", [P, NB]), sb("tmp", [P, NB])
        ps = mem.enter_context(nc.psum_tensor(tag + "ps", [P, 2, 512], F32))
        s = {n: phase_sem(nc, mem, (tag + n)) for n in ("dve", "mm", "feed", "root", "rooted")}
        with nc.Block() as block:
            @block.vector
            def _(dve):
                ch = Chain(dve, s["dve"])
                dve.wait_ge(s["mm"], 1)
                ch.then(dve.tensor_copy(norm[:, :, 2], ps[:, 0, 0:NB]))
                ch.then(dve.tensor_tensor(dev[:, :], mv[:, :, 0], norm[:, :, 2], ALU.subtract))
                ch.then(dve.tensor_tensor(dev[:, :], dev[:, :], dev[:, :], ALU.mult))
                ch.then(dve.tensor_tensor(dev[:, :], dev[:, :], mv[:, :, 1], ALU.add))
                dve.sem_inc(s["feed"], 1)
                dve.wait_ge(s["mm"], 2)
                ch.then(dve.tensor_copy(var[:, :], ps[:, 1, 0:NB]))
                rstd_of(nc, dve, ch, s["root"], s["rooted"], var[:, :], rs[:, :], tmp[:, :])
                ch.then(dve.tensor_copy(norm[:, :, 0], rs[:, :]))
                ch.then(dve.scalar_tensor_tensor(norm[:, :, 1], rs[:, :], -1.0, norm[:, :, 2], ALU.mult, ALU.mult))

            @block.tensor
            def _(pe):
                nc.tensor.matmul(ps[:, 0, 0:NB], t["group_avg"][:, :], mv[:, :, 0], start=True, stop=True).then_inc(s["mm"], 1)
                pe.wait_ge(s["feed"], 1)
                nc.tensor.matmul(ps[:, 1, 0:NB], t["group_avg"][:, :], dev[:, :], start=True, stop=True).then_inc(s["mm"], 1)

            @block.scalar
            def _(act):
                act.wait_ge(s["root"], 1)
                act.activation(tmp[:, :], var[:, :], ACT.Sqrt).then_inc(s["rooted"], 1)


CG = 8
NCG = C // CG


def spectrum_phase(nc, top, NB, x, io, bn, X):
    with Phase(nc) as mem:
        sb = lambda n, s: mem.enter_context(nc.sbuf_tensor("sp_" + n, s, F32))
        xin = sb("xin", [P, 4, 2, CG, W])
        fh = sb("fh", [P, 2, 64])
        fw = sb("fw", [P, 2, 2, 64])
        ident = sb("ident", [P, P])
        B = sb("B", [P, 2, 2, 2, 2, P])
        A = sb("A", [P, 2, 2, M1, C])
        psA = mem.enter_context(nc.psum_tensor("sp_psA", [P, 2, 2, 512], F32))
        psT = mem.enter_context(nc.psum_tensor("sp_psT", [P, 2, 2, 2, P], F32))
        psX = mem.enter_context(nc.psum_tensor("sp_psX", [P, NG * 64], F32))
        sem = lambda n: phase_sem(nc, mem, ("sp_" + n))
        small = sem("small")
        x_full, x_free_dve = [sem(f"x_full{i}") for i in range(4)], sem("x_free_dve")
        a_ready, b_copied, turned, t_copied, x_ready, x_copied = (sem("a_ready"), sem("b_copied"), sem("turned"), sem("t_copied"),
                                                                  sem("x_ready"), sem("x_copied"))

        def pipeline(eng, tile, turn, modes):
            def image(b, first):
                for k in range(NCG):
                    tile(b, k)
                    if k == 1 and not first:
                        modes(b - 1)
                    if k >= 1:
                        turn(b, k - 1)
                    elif not first:
                        turn(b - 1, NCG - 1)
            image(0, True)
            with eng.Fori(1, NB) as b:
                image(b, False)
            turn(NB - 1, NCG - 1)
            modes(NB - 1)

        with nc.Block() as block:
            @block.sync
            def _(sp):
                loads(sp, small, [(fh[:, :, :], io["dft_h"].rearrange("(t p) k -> p t k", p=P)),
                                  (fw[:, :, :, :], io["dft_w"].rearrange("(t p) a k -> p t a k", p=P)), (ident[:, :], io["ident"])])
                with sp.Fori(0, NB) as b:
                    for k in range(NCG):
                        sp.wait_ge(a_ready, b * NCG + k + 1)
                        sp.wait_ge(x_free_dve, b * NCG + k + 1)
                        for h in range(2):
                            sp.dma_start(xin[:, k, h, :, :],
                                         x[b, k * CG:(k + 1) * CG, h * P:(h + 1) * P, :].rearrange("c p w -> p c w")
                                         ).then_inc(x_full[k], 16)

            @block.tensor
            def _(pe):
                pe.wait_ge(small, 48)
                pe.sem_inc(a_ready, 4)
                pe.sem_inc(turned, 4)
                pe.sem_inc(x_ready, 1)

                def tile(b, k):
                    pe.wait_ge(x_full[k], 32 * b + 32)
                    pe.wait_ge(b_copied, b * NCG + k + 1)
                    for m in range(2):
                        for h in range(2):
                            for t in range(2):
                                last = nc.tensor.matmul(psA[64 * t:64 * t + 64, k % 2, m, :].rearrange("p (e w) -> p e w", e=2), fh[:, h, :],
                                                        xin[:, k, h, 4 * m + t:4 * m + t + 3:2, :],
                                                        start=(h == 0), stop=(h == 1), tile_position=(0, 64 * t))
                    last.then_inc(a_ready, 1)

                def turn(b, k):
                    pe.wait_ge(b_copied, b * NCG + k + 3)
                    for m in range(2):
                        pe.wait_ge(t_copied, (b * NCG + k) * 2 + m + 1)
                        for e in range(2):
                            for wh in range(2):
                                last = nc.tensor.transpose(psT[:, m, wh, e, :], B[:, k % 2, m, e, wh, :], ident[:, :])
                        last.then_inc(turned, 1)

                def modes(b):
                    pe.wait_ge(t_copied, b * (2 * NCG) + 2 * NCG + 2)
                    pe.wait_ge(x_copied, b + 1)
                    for g in range(NG):
                        n = 0
                        for wh in range(2):
                            for cs in range(2):
                                last = nc.tensor.matmul(psX[:, g * 64:(g + 1) * 64],
                                                        A[:, wh, cs, g * J:(g + 1) * J, :].rearrange("p j c -> p (j c)"),
                                                        fw[:, wh, cs, :], start=(n == 0), stop=(n == 3))
                                n += 1
                    last.then_inc(x_ready, 1)

                pipeline(pe, tile, turn, modes)

            @block.scalar
            def _(act):
                act.sem_inc(b_copied, 2)
                act.sem_inc(t_copied, 2)
                act.sem_inc(x_copied, 1)

                def tile(b, k):
                    act.wait_ge(a_ready, b * NCG + k + 5)
                    act.wait_ge(turned, (b * NCG + k) * 2 + 2)
                    act.activation(B[:, k % 2, :, :, :, :].rearrange("p m e h w -> p (m e h w)"),
                                   psA[:, k % 2, :, :].rearrange("p m n -> p (m n)"), ACT.Copy).then_inc(b_copied, 1)

                def turn(b, k):
                    if k == 0:
                        act.wait_ge(x_ready, b + 1)
                    for m in range(2):
                        act.wait_ge(turned, (b * NCG + k) * 2 + m + 5)
                        c = k * CG + 4 * m
                        act.activation(A[:, :, :, :, c:c + 4].rearrange("p h a k c -> p h c (a k)"),
                                       psT[:, m, :, :, :].rearrange("p h e (t n) -> p h (e t) n", t=2), ACT.Copy).then_inc(t_copied, 1)

                def modes(b):
                    act.wait_ge(x_ready, b + 2)
                    act.activation(X[:, b, :], psX[:, :], ACT.Copy).then_inc(x_copied, 1)

                pipeline(act, tile, turn, modes)

            @block.vector
            def _(dve):
                dve.sem_inc(x_free_dve, 4)
                with dve.Fori(0, NB) as b:
                    for k in range(NCG):
                        dve.wait_ge(x_full[k], 32 * b + 32)
                        for c in range(CG):
                            last = dve.bn_stats(bn[:, b, k * CG + c, :], xin[:, k, :, c, :])
                        last.then_inc(x_free_dve, 1)


def mixing_phase(nc, top, NB, io, X, norm, Y, maps):
    ZR, ZE = 96, MAPW * 2 * MAPW // 96
    KQ = P // C
    NQ = M2 // KQ
    with Phase(nc) as mem:
        sb = lambda n, s: mem.enter_context(nc.sbuf_tensor("mx_" + n, s, F32))
        coef = sb("coef", [P, 2, 2, NQ, P])
        p_re, p_im = sb("p_re", [P, KQ, C]), sb("p_im", [P, KQ, 2, C])
        W3 = sb("W3", [P, 2, KQ, NQ, 3, C])
        Xg = sb("Xg", [P, NB, 64])
        Xd = sb("Xd", [P, 2, 64, J, NB])
        own = sb("own", [P, J])
        Yg = sb("Yg", [J * NB, 2, 64, M2])
        zero = sb("zero", [ZR, ZE])
        psW = mem.enter_context(nc.psum_tensor("mx_psW", [P, 4, KQ, 128], F32))
        psY = mem.enter_context(nc.psum_tensor("mx_psY", [J * NB, 4, 8, 64], F32))
        sem = lambda n: phase_sem(nc, mem, ("mx_" + n))
        small, c_full, zeroed = sem("small"), [sem(f"c_full{i}") for i in range(2)], sem("zeroed")
        prep, w_ready, w_copied, spread = sem("prep"), sem("w_ready"), sem("w_copied"), sem("spread")
        border, border_out = sem("border"), sem("border_out")
        mixed, y_copied, stored = sem("mixed"), sem("y_copied"), [sem(f"stored{i}") for i in range(2)]
        with nc.Block() as block:
            @block.sync
            def _(sp):
                sp.wait_ge(zeroed, 2)
                pairs = [(own[:, :], io["quarter_att"])]
                for q in range(KQ):
                    r = slice(C * q, C * q + C)
                    pairs += [(p_re[r, q, :], io["proj_T"]), (p_im[r, q, 1, :], io["proj_T"])]
                loads(sp, small, pairs)
                with sp.Fori(0, NG // 2) as pair:
                    for u in range(2):
                        g = pair * 2 + u
                        sp.wait_ge(w_ready, g * NQ + NQ)
                        for a, n in enumerate(("coeff_real", "coeff_imag")):
                            sp.dma_start(coef[:, u, a, :, :],
                                         io[n][:, g, :, :, :].rearrange("r (q n) j c -> q r (n j c)", q=KQ)).then_inc(c_full[u], 16)

            @block.gpsimd
            def _(pool):
                pool.memset(zero[:, :], 0.0).then_inc(border, 1)
                pool.wait_ge(border, 1)
                with pool.Fori(0, NB) as b:
                    pool.dma_start(bass.AP(maps.tensor, b * (ZR * ZE), [[ZE, ZR], [1, ZE]]), zero[:, :]).then_inc(border_out, 16)
                pool.wait_ge(border_out, NB * 16)

            @block.vector
            def _(dve):
                dve.memset(p_re[:, :, :], 0.0).then_inc(zeroed, 1)
                dve.memset(p_im[:, :, :, :], 0.0).then_inc(zeroed, 1)
                ch = Chain(dve, prep)
                dve.wait_ge(small, 16 * (1 + 2 * KQ))
                ch.then(dve.tensor_scalar(p_im[:, :, 0, :], p_im[:, :, 1, :], -1.0, None, ALU.mult))
                ch.then(dve.scalar_tensor_tensor(X[0:C, :, 0], norm[0:C, :, 2], -float(HW), X[0:C, :, 0], ALU.mult, ALU.add))
                with dve.Fori(0, NG // 2) as pair:
                    for u in range(2):
                        g = pair * 2 + u
                        dve.wait_ge(mixed, g * 4 + 4)
                        for n in range(NQ):
                            dve.wait_ge(w_ready, g * NQ + 2 * NQ + n + 1)
                            dve.tensor_copy(W3[:, u, :, n, :, :].rearrange("p k a o -> p k (a o)"),
                                            psW[:, n % 4, :, 0:3 * C]).then_inc(w_copied, 1)
                        dve.tensor_tensor(Xg[:, :, :], X[:, :, bass.ds(g * 64, 64)],
                                          norm[:, :, 0].unsqueeze(2).to_broadcast([P, NB, 64]), ALU.mult).then_inc(spread, 1)
                        dve.wait_ge(spread, g * (J + 1) + 1)
                        for j in range(J):
                            dve.tensor_scalar(Xd[:, u, :, j, :], Xg[:, :, :].rearrange("p b e -> p e b"),
                                              own[:, j:j + 1], None, ALU.mult).then_inc(spread, 1)
                        dve.wait_ge(spread, g * (J + 1) + J + 1)

            @block.tensor
            def _(pe):
                pe.wait_ge(prep, 1)
                pe.sem_inc(w_ready, 2 * NQ)
                pe.sem_inc(mixed, 8)

                def weights(pair, u):
                    pe.wait_ge(c_full[u], pair * 32 + 32)
                    for n in range(NQ):
                        pe.wait_ge(w_copied, (pair * 2 + u) * NQ + n + 1)
                        nc.tensor.matmul(psW[:, n % 4, :, C:2 * C], coef[:, u, 0, n, :], p_re[:, :, :], start=True, stop=True)
                        nc.tensor.matmul(psW[:, n % 4, :, :].rearrange("p i (o v c) -> p i v o c", v=2, c=C)[:, :, 0, :, :],
                                         coef[:, u, 1, n, :], p_im[:, :, :, :], start=True, stop=True).then_inc(w_ready, 1)

                def modes(pair, u):
                    g = pair * 2 + u
                    pe.wait_ge(w_copied, g * NQ + NQ + 4)
                    pe.wait_ge(spread, g * (J + 1) + J + 1)
                    for e in range(4):
                        pe.wait_ge(y_copied, g * 4 + e + 1)
                        for i in range(8):
                            k2 = 8 * e + i
                            W = W3[:, u, k2 // NQ, k2 % NQ, :, :].rearrange("p a o -> p (a o)")
                            for a, w in ((0, W[:, C:3 * C]), (1, W[:, 0:2 * C])):
                                last = nc.tensor.matmul(psY[:, e, i, :], Xd[:, u, 32 * a + k2, :, :].rearrange("p j b -> p (j b)"), w,
                                                        start=(a == 0), stop=(a == 1))
                        last.then_inc(mixed, 1)

                weights(0, 0)
                with pe.Fori(0, NG // 2 - 1) as pair:
                    weights(pair, 1)
                    modes(pair, 0)
                    weights(pair + 1, 0)
                    modes(pair, 1)
                weights(NG // 2 - 1, 1)
                for u in range(2):
                    modes(NG // 2 - 1, u)

            @block.scalar
            def _(act):
                act.sem_inc(w_copied, 4)
                act.sem_inc(y_copied, 4)
                for u in range(2):
                    act.sem_inc(stored[u], 16 * J)
                with act.Fori(0, NG // 2) as pair:
                    for u in range(2):
                        g = pair * 2 + u
                        act.wait_ge(stored[u], pair * (16 * J) + 16 * J)
                        for e in range(4):
                            act.wait_ge(mixed, g * 4 + 8 + e + 1)
                            act.activation(Yg[:, u, :, 8 * e:8 * e + 8].rearrange("b o k -> b k o"),
                                           psY[:, e, :, :], ACT.Copy).then_inc(y_copied, 1)
                        act.wait_ge(y_copied, g * 4 + 8)
                        for j in range(J):
                            act.dma_start(Y[:, :, :, g * J + j, :].rearrange("b a o k -> b (a o) k"),
                                          Yg[j * NB:(j + 1) * NB, u, :, :]).then_inc(stored[u], 16)
                for u in range(2):
                    act.wait_ge(stored[u], 16 * J * (NG // 2 + 1))


def inverse_phase(nc, top, NB, x, io, Y, x1, bn):
    with Phase(nc) as mem:
        sb = lambda n, s: mem.enter_context(nc.sbuf_tensor("iv_" + n, s, F32))
        xin = sb("xin", [P, 2 * NCG, CG, 2, W])
        Yb = sb("Yb", [64, 2, C, 2, M2])
        Z = sb("Z", [P, 2, C // 2, H])
        eh = sb("eh", [64, H])
        fw = sb("fw", [P, 2, W])
        psZ = mem.enter_context(nc.psum_tensor("iv_psZ", [P, 2, 2, H], F32))
        psI = mem.enter_context(nc.psum_tensor("iv_psI", [P, 4, 2, W], F32))
        sem = lambda n: phase_sem(nc, mem, ("iv_" + n))
        passed = sem("passed")
        small = sem("small")
        x_full, x_out = [sem(f"x_full{i}") for i in range(2 * NCG)], [sem(f"x_out{i}") for i in range(2 * NCG)]
        y_full = [sem(f"y_full{i}") for i in range(2)]
        y_neg, z_ready, z_copied, i_ready, added, x_done = sem("y_neg"), sem("z_ready"), sem("z_copied"), sem("i_ready"), sem("added"), sem("x_done")
        tile_of = lambda v, b, k, h: v[b, k * CG:(k + 1) * CG, h * P:(h + 1) * P, :].rearrange("c p w -> p c w")
        with nc.Block() as block:
            @block.sync
            def _(sp):
                loads(sp, small, [(eh[:, :], io["idft_h"]), (fw[:, :, :], io["idft_w"].rearrange("p (a w) -> p a w", a=2))])

                def load_modes(b, u):
                    for a in range(2):
                        for v in range(2):
                            row = (a ^ v) * 32
                            sp.dma_start(Yb[row:row + 32, u, :, v, :], Y[b, a].rearrange("o k l -> k o l")).then_inc(y_full[u], 16)

                def load_image(b, u, pair):
                    for k in range(NCG):
                        slot = u * NCG + k
                        if pair is not None:
                            sp.wait_ge(x_out[slot], pair * 32)
                        for h in range(2):
                            sp.dma_start(xin[:, slot, :, h, :], tile_of(x, b, k, h)).then_inc(x_full[slot], 16)

                for u in range(2):
                    load_modes(u, u)
                    load_image(u, u, None)
                if NB > 2:
                    with sp.Fori(1, NB // 2) as pair:
                        for u in range(2):
                            sp.wait_ge(z_ready, (pair * 2 + u) * 8 - 8)
                            load_modes(pair * 2 + u, u)
                            load_image(pair * 2 + u, u, pair)

            @block.gpsimd
            def _(pool):
                with pool.Fori(0, NB // 2) as pair:
                    for u in range(2):
                        for k in range(NCG):
                            slot = u * NCG + k
                            wait_alone(pool, x_done, (pair * 2 + u) * NCG + k + 1, passed)
                            for h in range(2):
                                pool.dma_start(tile_of(x1, pair * 2 + u, k, h), xin[:, slot, :, h, :]).then_inc(x_out[slot], 16)
                for slot in range(2 * NCG):
                    pool.wait_ge(x_out[slot], 16 * NB)

            @block.tensor
            def _(pe):
                pe.wait_ge(small, 32)
                pe.sem_inc(i_ready, 17)

                def rows(b, u, n):
                    if n == 0:
                        pe.wait_ge(y_neg, b + 1)
                    pe.wait_ge(z_copied, b * 8 + n + 1)
                    for i in range(2):
                        op = 2 * n + i
                        last = nc.tensor.matmul(psZ[:, n % 2, i, :], Yb[:, u, 2 * op:2 * op + 2, :, :].rearrange("p o v k -> p (o v k)"),
                                                eh[:, :], start=True, stop=True)
                    last.then_inc(z_ready, 1)

                def image(b, u, final):
                    pe.wait_ge(z_copied, b * 8 + 10)
                    for op in range(C // 2):
                        pe.wait_ge(added, b * 16 + op + 1)
                        for h in range(2):
                            last = nc.tensor.matmul(psI[:, (2 * op) % 4 + h, :, :].rearrange("p o w -> p (o w)"), Z[:, u, op, h * P:(h + 1) * P],
                                                    fw[:, :, :].rearrange("p o w -> p (o w)"), start=True, stop=True)
                        last.then_inc(i_ready, 1)
                        if op % 2 == 1 and not final:
                            rows(b + 1, 1 - u, op // 2)

                for n in range(8):
                    rows(0, 0, n)
                if NB > 2:
                    with pe.Fori(0, NB // 2 - 1) as pair:
                        for u in range(2):
                            image(pair * 2 + u, u, False)
                for u in range(2):
                    image(NB - 2 + u, u, u == 1)

            @block.scalar
            def _(act):
                act.sem_inc(z_copied, 2)
                with act.Fori(0, NB // 2) as pair:
                    for u in range(2):
                        b = pair * 2 + u
                        act.wait_ge(i_ready, b * 16 + 1)
                        for n in range(8):
                            act.wait_ge(z_ready, b * 8 + n + 1)
                            act.activation(Z[:, u, 2 * n:2 * n + 2, :], psZ[:, n % 2, :, :], ACT.Copy).then_inc(z_copied, 1)

            @block.vector
            def _(dve):
                dve.sem_inc(added, 2)

                def negate(pair, u):
                    dve.wait_ge(y_full[u], pair * 64 + 64)
                    dve.tensor_scalar(Yb[32:64, u, :, 0, :], Yb[32:64, u, :, 0, :], -1.0, None, ALU.mult).then_inc(y_neg, 1)

                def image(pair, u):
                    b = pair * 2 + u
                    for k in range(NCG):
                        slot = u * NCG + k
                        dve.wait_ge(x_full[slot], pair * 32 + 32)
                        for i in range(CG // 2):
                            op = k * (CG // 2) + i
                            dve.wait_ge(i_ready, b * 16 + op + 18)
                            bank = (2 * op) % 4
                            xs = xin[:, slot, 2 * i:2 * i + 2, :, :]
                            dve.tensor_tensor(xs, xs, psI[:, bank:bank + 2, :, :].rearrange("p h c w -> p c h w"), ALU.add).then_inc(added, 1)
                        dve.wait_ge(added, b * 16 + (k + 1) * (CG // 2) + 2)
                        for c in range(CG):
                            last = dve.bn_stats(bn[:, b, k * CG + c, :], xin[:, slot, c, :, :])
                        last.then_inc(x_done, 1)

                negate(0, 0)
                if NB > 2:
                    with dve.Fori(0, NB // 2 - 1) as pair:
                        negate(pair, 1)
                        image(pair, 0)
                        negate(pair + 1, 0)
                        image(pair, 1)
                negate(NB // 2 - 1, 1)
                for u in range(2):
                    image(NB // 2 - 1, u)


LN = 4
LE = LN * W
NCH = QR // LN


def scan_chunk(dve, n, xn, gate, S, M, step):
    done = (n + 2) * 8
    fwd, bwd = slice(None), slice(None, None, -1)
    flat = lambda a, r: a[:, r]
    for d, r in ((0, fwd), (1, bwd)):
        dve.tensor_tensor_scan(flat(S[:, d, :], r), flat(gate[d], r), flat(xn, r), 0.0, ALU.mult, ALU.add).then_inc(step, 1)
    for d, at in ((0, 0), (1, W - 1)):
        dve.wait_ge(step, done + 1 + d)
        dve.memset(S[:, d, :].rearrange("p (l k) -> p l k", k=W)[:, :, at:at + 1], 0.0).then_inc(step, 1)
    for d, r in ((0, fwd), (1, bwd)):
        dve.wait_ge(step, done + 3 + d)
        last = dve.tensor_tensor_scan(flat(M[:, d, :], r), flat(gate[d], r), flat(S[:, d, :], r), 0.0, ALU.mult, ALU.min)
        last.then_inc(step, 1)
    for d, at in ((0, 0), (1, W - 1)):
        dve.wait_ge(step, done + 5 + d)
        first = lambda a: a.rearrange("p (l k) -> p l k", k=W)[:, :, at:at + 1]
        dve.tensor_copy(first(S[:, d, :]), first(xn)).then_inc(step, 1)


def mix_directions(nc, ps, S, M, w_pos, w_neg, first, extra=None):
    for k in range(LE // 512):
        e = slice(k * 512, (k + 1) * 512)
        out = ps[:, k, :]
        if extra is not None:
            rows = 512 // W
            nc.tensor.matmul(out.rearrange("p (r q l) -> p r q l", q=Q, l=QR), extra[0],
                             extra[1][:, k * rows:(k + 1) * rows, :, :], start=True, stop=False)
        for d in range(2):
            nc.tensor.matmul(out, w_pos[:, first + d, :], S[:, d, e], start=(d == 0 and extra is None), stop=False)
            last = nc.tensor.matmul(out, w_neg[:, first + d, :], M[:, d, e], start=False, stop=(d == 1))
    return last


STORE_AT = (2, 3, 4, 5)
LOAD_AT = (6, 8, 10, 12)


def vertical_phase(nc, top, NB, x1, gates, t, norm, pb):
    with Phase(nc) as mem:
        sb = lambda n, s: mem.enter_context(nc.sbuf_tensor("ve_" + n, s, F32))
        img = sb("img", [P, 2, H, QR])
        xn, gt = sb("xn", [P, 2, LE]), sb("gate", [P, 4, 2, LE])
        S, M = sb("S", [P, 2, 2, LE]), sb("M", [P, 2, 2, LE])
        coef = sb("coef", [P, 2, 3])
        ps = mem.enter_context(nc.psum_tensor("ve_ps", [P, 4, 2, 512], F32))
        sem = lambda n: phase_sem(nc, mem, ("ve_" + n))
        img_full, img_out = [sem(f"img_full{i}") for i in range(2)], [sem(f"img_out{i}") for i in range(2)]
        gate_full = [sem(f"gate_full{i}") for i in range(4)]
        coef_ready, xn_ready, step, mixed, evac = sem("coef_ready"), sem("xn_ready"), sem("step"), sem("mixed"), sem("evac")
        
        def move(sp, b, q, u, store, sem):
            tile = img[q:q + P - Q + 1:Q, u, :, :]
            if store:
                sp.dma_start(pb[b, :, :, q].rearrange("c s r l -> c s (r l)"), tile.rearrange("c (s r) l -> c s (r l)", s=Q)).then_inc(sem, 16)
            else:
                sp.dma_start(tile, x1[b, :, :, q * QR:(q + 1) * QR]).then_inc(sem, 16)

        with nc.Block() as block:
            @block.sync
            def _(sp):
                def load_gates(slot, k):
                    for d in range(2):
                        sp.dma_start(gt[:, slot, d, :],
                                     bass.AP(gates.tensor, (2 + d) * HW + k * LE, [[0, C], [HW // Q, Q], [1, LE]])
                                     ).then_inc(gate_full[slot], 16)

                def image(b, u, first, last):
                    for k in range(NCH):
                        sp.wait_ge(step, (b * NCH + k) * 8 + 16)
                        load_gates((k + 3) % 4, (k + 3) % NCH)
                        if not first and k in STORE_AT:
                            sp.wait_ge(evac, b * NCH + 4)
                            move(sp, b - 1, STORE_AT.index(k), 1 - u, True, img_out[1 - u])
                        if not last and k in LOAD_AT:
                            if not first:
                                sp.wait_ge(img_out[1 - u], (b + u) * 32)
                            move(sp, b + 1, LOAD_AT.index(k), 1 - u, False, img_full[1 - u])

                for q in range(Q):
                    move(sp, 0, q, 0, False, img_full[0])
                for k in range(3):
                    load_gates(k, k)
                image(0, 0, True, False)
                image(1, 1, False, False)
                if NB > 4:
                    with sp.Fori(1, NB // 2 - 1) as pair:
                        for u in range(2):
                            image(pair * 2 + u, u, False, False)
                image(NB - 2, 0, False, False)
                image(NB - 1, 1, False, True)
                sp.wait_ge(evac, NB * NCH + 4)
                for q in range(Q):
                    move(sp, NB - 1, q, 1, True, img_out[1])
                for u in range(2):
                    sp.wait_ge(img_out[u], 64 * (NB // 2))
                for slot in range(4):
                    sp.wait_ge(gate_full[slot], 32 * (NB * NCH // 4 + (slot < 3)))

            @block.scalar
            def _(act):
                act.sem_inc(evac, 4)

                def unload(b, u, j):
                    act.wait_ge(mixed, b * NCH + j + 3)
                    act.activation(img[:, u, :, j * LN:(j + 1) * LN].rearrange("p h l -> p l h"),
                                   ps[:, j % 4, :, :].rearrange("p k (l r) -> p (k l) r", r=H), ACT.Copy).then_inc(evac, 1)

                def image(b, u, first):
                    if not first:
                        act.wait_ge(mixed, b * NCH)
                    act.activation(coef[:, u, :], norm[:, b, :], ACT.Copy).then_inc(coef_ready, 1)
                    act.wait_ge(coef_ready, b + 1)
                    act.wait_ge(img_full[u], b * 32 + (64 - 32 * u))
                    for k in range(NCH):
                        act.wait_ge(step, (b * NCH + k) * 8 + 8)
                        act.activation(xn[:, k % 2, :].rearrange("p (l r) -> p l r", r=H),
                                       img[:, u, :, k * LN:(k + 1) * LN].rearrange("p h l -> p l h"),
                                       ACT.Identity, scale=coef[:, u, 0:1], bias=coef[:, u, 1:2]).then_inc(xn_ready, 1)
                        if k >= 2:
                            unload(b, u, k - 2)
                        elif not first:
                            unload(b - 1, 1 - u, NCH - 2 + k)

                image(0, 0, True)
                image(1, 1, False)
                with act.Fori(1, NB // 2) as pair:
                    for u in range(2):
                        image(pair * 2 + u, u, False)
                for k in range(2):
                    unload(NB - 1, 1, NCH - 2 + k)

            @block.vector
            def _(dve):
                dve.sem_inc(step, 16)
                with dve.Fori(0, NB // 2) as pair:
                    for k in range(2 * NCH):
                        n = pair * (2 * NCH) + k
                        dve.wait_ge(xn_ready, n + 1)
                        dve.wait_ge(gate_full[k % 4], pair * (16 * NCH) + 32 * (k // 4 + 1))
                        dve.wait_ge(mixed, n + 1)
                        scan_chunk(dve, n, xn[:, k % 2, :], [gt[:, k % 4, d, :] for d in range(2)],
                                   S[:, k % 2, :, :], M[:, k % 2, :, :], step)

            @block.tensor
            def _(pe):
                pe.sem_inc(mixed, 2)
                with pe.Fori(0, NB) as b:
                    for k in range(NCH):
                        n = b * NCH + k
                        pe.wait_ge(step, n * 8 + 24)
                        pe.wait_ge(evac, n + 1)
                        mix_directions(nc, ps[:, k % 4, :, :], S[:, k % 2, :, :], M[:, k % 2, :, :],
                                       t["w_dir"], t["w_neg"], 2).then_inc(mixed, 1)


def horizontal_phase(nc, top, NB, x1, pb, gates, t, norm, x2, mv):
    with Phase(nc) as mem:
        sb = lambda n, s: mem.enter_context(nc.sbuf_tensor("ho_" + n, s, F32))
        gt = sb("gate", [P, 2, HW // Q])
        x_in, pb_in = sb("x_in", [P, 4, LE]), sb("pb_in", [P, 2, Q, LN * QR])
        xn, y = sb("xn", [P, 2, LE]), sb("y", [P, 2, LE])
        S, M = sb("S", [P, 2, 2, LE]), sb("M", [P, 2, 2, LE])
        coef = sb("coef", [P, 3])
        bns = sb("bns", [P, 2 * NCH, 6])
        agg = sb("agg", [P, 2])
        ps = mem.enter_context(nc.psum_tensor("ho_ps", [P, 4, 2, 512], F32))
        sem = lambda n: phase_sem(nc, mem, ("ho_" + n))
        passed = sem("passed")
        y_out = [sem(f"y_out{i}") for i in range(2)]
        GP = 4
        gate_full, coef_ready = [sem(f"gate_full{i}") for i in range(GP)], sem("coef_ready")
        x_full, pb_full = [sem(f"x_full{i}") for i in range(4)], [sem(f"pb_full{i}") for i in range(2)]
        xn_ready, step, mixed, evac, added, stat, agg_done = (sem("xn_ready"), sem("step"), sem("mixed"), sem("evac"), sem("added"), sem("stat"), sem("agg"))
        part = lambda a, b, k: a[b].rearrange("c (q r) w -> (c q) (r w)", q=Q)[:, k * LE:(k + 1) * LE]
        with nc.Block() as block:
            @block.sync
            def _(sp):
                def load_gates(i):
                    n = HW // Q // GP
                    for d in range(2):
                        sp.dma_start(gt[:, d, i * n:(i + 1) * n],
                                     bass.AP(gates.tensor, d * HW + i * n, [[0, C], [HW // Q, Q], [1, n]])).then_inc(gate_full[i], 16)

                def image(b, first):
                    for k in range(NCH):
                        if first and k % (NCH // GP) == 0:
                            load_gates(k // (NCH // GP))
                        sp.wait_ge(stat, b * NCH + k + 1)
                        sp.dma_start(x_in[:, k % 4, :], part(x1, b, k)).then_inc(x_full[k % 4], 16)
                        sp.wait_ge(mixed, b * NCH + k + 1)
                        sp.dma_start(pb_in[:, k % 2, :, :], pb[b].rearrange("c s q r l -> (c s) q (r l)")[:, :, k * LN * QR:(k + 1) * LN * QR]).then_inc(pb_full[k % 2], 16)

                image(0, True)
                with sp.Fori(1, NB) as b:
                    image(b, False)

            @block.scalar
            def _(act):
                act.sem_inc(evac, 4)
                act.sem_inc(xn_ready, 1)

                for out in y_out:
                    act.sem_inc(out, 16)

                def store(b, k):
                    act.wait_ge(added, b * NCH + k + 1)
                    act.dma_start(part(x2, b, k), y[:, k % 2, :]).then_inc(y_out[k % 2], 16)

                def rectify(b, k):
                    m = b * NCH + k
                    act.wait_ge(mixed, m + 3)
                    act.wait_ge(y_out[k % 2], b * (8 * NCH) + 16 * (k // 2 + 1))
                    act.wait_ge(stat, m + 3)
                    act.activation(y[:, k % 2, :], ps[:, k % 4, :, :].rearrange("p k n -> p (k n)"), ACT.Relu,
                                   bias=t["bias1"][:, 0:1]).then_inc(evac, 1)

                def image(b, first):
                    act.wait_ge(xn_ready, b * NCH + 1)
                    act.activation(coef[:, :], norm[:, b, :], ACT.Copy).then_inc(coef_ready, 1)
                    act.wait_ge(coef_ready, b + 1)
                    for k in range(NCH):
                        n = b * NCH + k
                        act.wait_ge(x_full[k % 4], b * (4 * NCH) + 16 * (k // 4 + 1))
                        act.wait_ge(step, n * 8 + 8)
                        act.activation(xn[:, k % 2, :], x_in[:, k % 4, :], ACT.Identity,
                                       scale=coef[:, 0:1], bias=coef[:, 1:2]).then_inc(xn_ready, 1)
                        if k >= 3:
                            store(b, k - 3)
                        elif not first:
                            store(b - 1, NCH - 3 + k)
                        if k >= 2:
                            rectify(b, k - 2)
                        elif not first:
                            rectify(b - 1, NCH - 2 + k)

                image(0, True)
                with act.Fori(1, NB) as b:
                    image(b, False)
                for k in (NCH - 2, NCH - 1):
                    store(NB - 1, k - 1)
                    rectify(NB - 1, k)
                store(NB - 1, NCH - 1)
                for out in y_out:
                    act.wait_ge(out, NB * (8 * NCH) + 16)

            @block.vector
            def _(dve):
                dve.sem_inc(agg_done, 1)
                dve.sem_inc(stat, 4)
                dve.sem_inc(step, 16)

                def add(b, k):
                    m = b * NCH + k
                    dve.wait_ge(evac, m + 5)
                    dve.tensor_tensor(y[:, k % 2, :], y[:, k % 2, :], x_in[:, k % 4, :], ALU.add).then_inc(added, 1)
                    dve.wait_ge(added, m + 1)
                    if k == 0:
                        dve.wait_ge(agg_done, 2 * b + 1)
                    for i in range(2):
                        last = dve.bn_stats(bns[:, 2 * k + i, :], y[:, k % 2, i * 512:(i + 1) * 512])
                    last.then_inc(stat, 1)

                def aggregate(b):
                    wait_alone(dve, stat, b * NCH + NCH + 4, passed)
                    dve.bn_aggr(agg[:, :], bns[:, :, :].rearrange("p n s -> p (n s)")).then_inc(agg_done, 1)
                    dve.wait_ge(agg_done, 2 * b + 2)
                    dve.tensor_copy(mv[:, b, :], agg[:, :]).then_inc(agg_done, 1)

                def image(b, first):
                    for k in range(NCH):
                        n = b * NCH + k
                        if first and k % (NCH // GP) == 0:
                            dve.wait_ge(gate_full[k // (NCH // GP)], 32)
                        dve.wait_ge(xn_ready, n + 2)
                        dve.wait_ge(mixed, n + 1)
                        scan_chunk(dve, n, xn[:, k % 2, :], [gt[:, d, k * LE:(k + 1) * LE] for d in range(2)],
                                   S[:, k % 2, :, :], M[:, k % 2, :, :], step)
                        if k >= 2:
                            add(b, k - 2)
                        elif not first:
                            add(b - 1, NCH - 2 + k)
                            if k == 1:
                                aggregate(b - 1)

                image(0, True)
                with dve.Fori(1, NB) as b:
                    image(b, False)
                for k in (NCH - 2, NCH - 1):
                    add(NB - 1, k)
                aggregate(NB - 1)

            @block.tensor
            def _(pe):
                pe.sem_inc(mixed, 2)
                with pe.Fori(0, NB) as b:
                    for k in range(NCH):
                        n = b * NCH + k
                        pe.wait_ge(step, n * 8 + 24)
                        pe.wait_ge(pb_full[k % 2], b * (8 * NCH) + 16 * (k // 2 + 1))
                        pe.wait_ge(evac, n + 1)
                        mix_directions(nc, ps[:, k % 4, :, :], S[:, k % 2, :, :], M[:, k % 2, :, :],
                                       t["w_dir"], t["w_neg"], 0, (t["ident"][:, :], pb_in[:, k % 2, :, :].rearrange("p q (r l) -> p r q l", l=QR))).then_inc(mixed, 1)


DY = 3
CJ = 8
JC = C // CJ
RT = 4
RE = RT * W


def kernels_phase(nc, top, NB, mv, norm, io, kern, mean3):
    with Phase(nc) as mem:
        sb = lambda n, s: mem.enter_context(nc.sbuf_tensor("kn_" + n, s, F32))
        w1, b1 = sb("w1", [P, P]), sb("b1", [P, 1])
        w2, b2, ones = sb("w2", [P, 288]), sb("b2", [1, 288]), sb("ones", [1, NB])
        w2q, b2q = sb("w2q", [P, 12, 3, CJ, Q]), sb("b2q", [1, 12, 3, CJ, Q])
        sel, centre = sb("sel", [P, JC, 96]), sb("centre", [96, 12])
        pooled, hid = sb("pooled", [P, NB]), sb("hid", [P, NB])
        rs3 = sb("rs3", [96, NB, JC])
        ps = mem.enter_context(nc.psum_tensor("kn_ps", [P, 4, 512], F32))
        s = {n: phase_sem(nc, mem, ("kn_" + n)) for n in ("small", "dve", "pooled", "mm", "hid", "wide")}
        with nc.Block() as block:
            @block.sync
            def _(sp):
                loads(sp, s["small"], [
                    (w1[:, :], bass.AP(io["mlp_w1"].tensor, 0, [[P, C], [0, Q], [1, P]])),
                    (b1[:, :], io["mlp_b1"]), (w2[:, :], io["mlp_w2"]), (b2[:, :], io["mlp_b2"]),
                    (sel[:, :, :], io["select_96"].rearrange("p (j m) -> p j m", m=96)), (centre[:, :], io["centre_96"])])

            @block.vector
            def _(dve):
                ch = Chain(dve, s["dve"])
                dve.wait_ge(s["small"], 96)
                dve.memset(ones[:, :], 1.0).then_inc(s["wide"], 1)
                for j in range(JC):
                    for dx in range(3):
                        for src, dst, n in ((w2, w2q, P), (b2, b2q, 1)):
                            v = src[:, 72 * j:72 * j + 72].rearrange("p (c y x) -> p y c x", y=3, x=3)[:, :, :, dx]
                            dve.tensor_copy(dst[:, 3 * j + dx, :, :, :], v.unsqueeze(3).to_broadcast([n, 3, CJ, Q])).then_inc(s["wide"], 1)
                ch.then(dve.tensor_tensor(pooled[:, :], mv[:, :, 0], norm[:, :, 2], ALU.subtract))
                ch.then(dve.scalar_tensor_tensor(pooled[:, :], pooled[:, :], 1.0 / Q, norm[:, :, 0], ALU.mult, ALU.mult))
                dve.sem_inc(s["pooled"], 1)
                dve.wait_ge(s["mm"], 2)
                for j in range(JC):
                    ch.then(dve.tensor_copy(mean3[:, :, j], ps[0:96, 1, j * 64:j * 64 + NB]))
                    ch.then(dve.tensor_copy(rs3[:, :, j], ps[0:96, 2, j * 64:j * 64 + NB]))
                dve.wait_ge(s["mm"], 3)
                raw = ps[0:96, 3, 0:12 * NB].rearrange("p (j x b) -> p b j x", j=JC, x=3)
                for j in range(JC):
                    ch.then(dve.tensor_tensor(kern[:, :, j, :], raw[:, :, j, :],
                                              rs3[:, :, j].unsqueeze(2).to_broadcast([96, NB, 3]), ALU.mult))
                    ch.then(dve.tensor_tensor(kern[:, :, j, :], kern[:, :, j, :],
                                              centre[:, 3 * j:3 * j + 3].unsqueeze(1).to_broadcast([96, NB, 3]), ALU.add))

            @block.tensor
            def _(pe):
                pe.wait_ge(s["small"], 96)
                pe.wait_ge(s["pooled"], 1)
                nc.tensor.matmul(ps[:, 0, 0:NB], w1[:, :], pooled[:, :], start=True, stop=True).then_inc(s["mm"], 1)
                for j in range(JC):
                    nc.tensor.matmul(ps[0:96, 1, j * 64:j * 64 + NB], sel[:, j, :], norm[:, :, 2], start=True, stop=True)
                    last = nc.tensor.matmul(ps[0:96, 2, j * 64:j * 64 + NB], sel[:, j, :], norm[:, :, 0], start=True, stop=True)
                last.then_inc(s["mm"], 1)
                pe.wait_ge(s["hid"], 1)
                pe.wait_ge(s["wide"], 25)
                for n in range(12):
                    out = ps[0:96, 3, n * NB:(n + 1) * NB]
                    nc.tensor.matmul(out, w2q[:, n, :, :, :].rearrange("p y c q -> p (y c q)"), hid[:, :], start=True, stop=False)
                    last = nc.tensor.matmul(out, b2q[:, n, :, :, :].rearrange("p y c q -> p (y c q)"), ones[:, :], start=False, stop=True)
                last.then_inc(s["mm"], 1)

            @block.scalar
            def _(act):
                act.wait_ge(s["mm"], 1)
                act.activation(hid[:, :], ps[:, 0, 0:NB], ACT.Relu, bias=b1[:, 0:1]).then_inc(s["hid"], 1)


def depthwise_phase(nc, top, NB, x2, kern, mean3, io, norm, x3, mv):
    NT = QR // RT
    with Phase(nc) as mem:
        sb = lambda n, s: mem.enter_context(nc.sbuf_tensor("dw_" + n, s, F32))
        tile = sb("tile", [P, 4, JC, RT, W])
        out = sb("out", [P, 4, RE])
        eye = sb("eye", [96, 32])
        inside = sb("inside", [96, 2])
        diag = sb("diag", [P, 2, 12, 32])
        bns, agg = sb("bns", [P, 2 * NT, 6]), sb("agg", [P, 2])
        mean_b, mean_o = sb("mean_b", [96, 2, JC]), sb("mean_o", [P, 2, 1])
        ps = mem.enter_context(nc.psum_tensor("dw_ps", [P, 4, 2, 512], F32))
        sem = lambda n: phase_sem(nc, mem, ("dw_" + n))
        passed = sem("passed")
        small, diag_ready, centred, conved, evac, stat = sem("small"), sem("diag_ready"), sem("centred"), sem("conved"), sem("evac"), sem("stat")
        agg_done, filled, mean_ready, prep = sem("agg"), sem("filled"), sem("mean_ready"), sem("prep")
        t_full, o_out = [sem(f"t_full{i}") for i in range(4)], [sem(f"o_out{i}") for i in range(4)]
        with nc.Block() as block:
            @block.sync
            def _(sp):
                loads(sp, small, [(eye[:, :], io["eye_96"]), (inside[:, :], io["inside_96"])])
                with sp.Fori(0, NB) as b:
                    for k in range(NT):
                        sp.wait_ge(conved, b * NT + k + 1)
                        for dy in range(DY):
                            src = bass.AP(x2.tensor, (b * C * HW) + W + (k * RT + dy - 1) * W,
                                          [[HW // Q, 32], [CJ * HW, JC], [1, RE]])
                            sp.dma_start(tile[32 * dy:32 * dy + 32, k % 4, :, :, :].rearrange("p j r w -> p j (r w)"), src
                                         ).then_inc(t_full[k % 4], 16)

            @block.vector
            def _(dve):
                dve.wait_ge(small, 32)
                dve.sem_inc(stat, 4)
                dve.sem_inc(agg_done, 1)
                dve.memset(tile[96:P, :, :, :, :].rearrange("p s j r w -> p (s j r w)"), 0.0).then_inc(filled, 1)
                dve.memset(diag[96:P, :, :, :].rearrange("p u n m -> p (u n m)"), 0.0).then_inc(filled, 1)

                def count(b, k):
                    dve.wait_ge(evac, b * NT + k + 5)
                    if k == 0:
                        dve.wait_ge(agg_done, 2 * b + 1)
                    for i in range(2):
                        last = dve.bn_stats(bns[:, 2 * k + i, :], out[:, k % 4, i * 512:(i + 1) * 512])
                    last.then_inc(stat, 1)

                def aggregate(b):
                    wait_alone(dve, stat, b * NT + NT + 4, passed)
                    dve.bn_aggr(agg[:, :], bns[:, :, :].rearrange("p n s -> p (n s)")).then_inc(agg_done, 1)
                    dve.wait_ge(agg_done, 2 * b + 2)
                    dve.tensor_copy(mv[:, b, :], agg[:, :]).then_inc(agg_done, 1)

                def image(b, u, first):
                    dve.wait_ge(conved, b * NT + 1)
                    dve.tensor_tensor(diag[0:96, u, :, :], eye[:, :].unsqueeze(1).to_broadcast([96, 12, 32]),
                                      kern[:, b, :, :].rearrange("p j x -> p (j x)").unsqueeze(2).to_broadcast([96, 12, 32]),
                                      ALU.mult).then_inc(diag_ready, 1)
                    dve.tensor_copy(mean_b[:, u, :], mean3[:, b, :]).then_inc(prep, 1)
                    dve.wait_ge(prep, b + 1)
                    for k in range(NT):
                        n = b * NT + k
                        dve.wait_ge(t_full[k % 4], b * (12 * NT) + 48 * (k // 4 + 1))
                        for j in range(JC):
                            part = tile[0:96, k % 4, j, :, :].rearrange("p r w -> p (r w)")
                            last = dve.tensor_scalar(part, part, mean_b[:, u, j:j + 1], None, ALU.subtract)
                        last.then_inc(centred, 1)
                        for edge, dy, row in ((0, 0, 0), (NT - 1, 2, RT - 1)):
                            if k == edge:
                                dve.wait_ge(centred, n + 1 + 2 * b + (1 if k else 0))
                                e = tile[32 * dy:32 * dy + 32, k % 4, :, row, :]
                                dve.tensor_scalar(e, e, inside[32 * dy:32 * dy + 32, edge > 0:(edge > 0) + 1],
                                                  None, ALU.mult).then_inc(centred, 1)
                        if k >= 2:
                            count(b, k - 2)
                        elif not first:
                            count(b - 1, NT - 2 + k)
                            if k == 1:
                                aggregate(b - 1)

                for u in range(2):
                    image(u, u, u == 0)
                with dve.Fori(1, NB // 2) as pair:
                    for u in range(2):
                        image(pair * 2 + u, u, False)
                for k in (NT - 2, NT - 1):
                    count(NB - 1, k)
                aggregate(NB - 1)

            @block.tensor
            def _(pe):
                pe.sem_inc(conved, 4)
                pe.wait_ge(filled, 2)
                with pe.Fori(0, NB // 2) as pair:
                    for u in range(2):
                        b = pair * 2 + u
                        pe.wait_ge(diag_ready, b + 1)
                        for k in range(NT):
                            n = b * NT + k
                            pe.wait_ge(centred, n + 2 + 2 * b + (1 if k == NT - 1 else 0))
                            pe.wait_ge(evac, n + 1)
                            for h in range(2):
                                for i, dx in enumerate((1, 0, 2)):
                                    w0, w1 = max(0, 1 - dx), min(W, W + 1 - dx)
                                    for j in range(JC):
                                        o = ps[32 * j:32 * j + 32, k % 4, h, :].rearrange("p (r w) -> p r w", w=W)
                                        last = nc.tensor.matmul(o[:, :, w0:w1], diag[:, u, 3 * j + dx, :],
                                                                tile[:, k % 4, j, 2 * h:2 * h + 2, w0 + dx - 1:w1 + dx - 1],
                                                                start=(i == 0), stop=(i == 2), tile_position=(0, 32 * j))
                            last.then_inc(conved, 1)

            @block.scalar
            def _(act):
                act.sem_inc(evac, 4)
                for done in o_out:
                    act.sem_inc(done, 16)
                with act.Fori(0, NB // 2) as pair:
                    for u in range(2):
                        b = pair * 2 + u
                        act.wait_ge(evac, b * NT + 4)
                        act.activation(mean_o[:, u, :], norm[:, b, 2:3], ACT.Copy).then_inc(mean_ready, 1)
                        act.wait_ge(mean_ready, b + 1)
                        for k in range(NT):
                            act.wait_ge(conved, b * NT + k + 5)
                            act.wait_ge(o_out[k % 4], b * (4 * NT) + 16 * (k // 4 + 1))
                            act.wait_ge(stat, b * NT + k + 1)
                            act.activation(out[:, k % 4, :], ps[:, k % 4, :, :].rearrange("p k n -> p (k n)"), ACT.Identity,
                                           bias=mean_o[:, u, :]).then_inc(evac, 1)
                            act.wait_ge(evac, b * NT + k + 5)
                            act.dma_start(x3[b].rearrange("c (q r) w -> (c q) (r w)", q=Q)[:, k * RE:(k + 1) * RE],
                                          out[:, k % 4, :]).then_inc(o_out[k % 4], 16)
                for done in o_out:
                    act.wait_ge(done, NB * (4 * NT) + 16)


def gate_phase(nc, top, NB, x3, io, t, norm, fs, maps):
    NT = QR // RT
    with Phase(nc) as mem:
        sb = lambda n, s: mem.enter_context(nc.sbuf_tensor("ga_" + n, s, F32))
        x_in, xn, prod, f = sb("x_in", [P, 4, RE]), sb("xn", [P, 4, RE]), sb("prod", [P, 2, RE]), sb("f", [P, 4, RE])
        rmax, rsum = sb("rmax", [P, 2, RT // 2, W]), sb("rsum", [P, 2, RT // 2, W])
        pmax, psumm, gate = sb("pmax", [P, 2, RE // 4]), sb("psum", [P, 2, RE // 4]), sb("gate", [P, 2, RE // 4])
        coef = sb("coef", [P, 3])
        ca = sb("ca", [2 * C, 2, 512])
        cmT = sb("cmT", [P, 2, Q, QR])
        cm = sb("cm", [P, 2, 2, P])
        psF = mem.enter_context(nc.psum_tensor("ga_psF", [P, 2, 512], F32))
        psT = mem.enter_context(nc.psum_tensor("ga_psT", [P, 2, RT, P], F32))
        psC = mem.enter_context(nc.psum_tensor("ga_psC", [2 * C, 512], F32))
        psM = mem.enter_context(nc.psum_tensor("ga_psM", [P, 2, 2, P], F32))
        sem = lambda n: phase_sem(nc, mem, ("ga_" + n))
        x_full = [sem(f"x_full{i}") for i in range(4)]
        f_out, ca_out = [sem(f"f_out{i}") for i in range(4)], [sem(f"ca_out{i}") for i in range(2)]
        coef_ready, xn_ready, pool_step, sig, gated = sem("coef_ready"), sem("xn_ready"), sem("pool_step"), sem("sig"), sem("gated")
        conved, f_ready, turned, maxed, ca_ready, cm_turned, cm_ready, cm_out = (sem("conved"), sem("f_ready"), sem("turned"), sem("maxed"),
                                                                               sem("ca_ready"), sem("cm_turned"), sem("cm_ready"), sem("cm_out"))
        part = lambda a, b, k: a[b].rearrange("c (q r) w -> (c q) (r w)", q=Q)[:, k * RE:(k + 1) * RE]
        plane = MAPW * 2 * MAPW

        def lagged(b, k, lag, first):
            j = k - lag
            if 0 <= j < NT:
                return b, j
            return (b - 1, NT + j) if j < 0 and not first else None

        def steps(eng, step, flush):
            for k in range(NT):
                step(0, k, True)
            with eng.Fori(1, NB) as b:
                for k in range(NT):
                    step(b, k, False)
            for k in range(NT, NT + flush):
                step(NB - 1, k, False)

        with nc.Block() as block:
            @block.sync
            def _(sp):
                with sp.Fori(0, NB) as b:
                    for k in range(NT):
                        sp.wait_ge(xn_ready, b * NT + k + 1)
                        sp.dma_start(x_in[:, k % 4, :], part(x3, b, k)).then_inc(x_full[k % 4], 16)

            @block.scalar
            def _(act):
                act.sem_inc(xn_ready, 4)
                act.sem_inc(ca_ready, 2)
                act.sem_inc(f_ready, 1)
                act.sem_inc(cm_ready, 1)
                act.sem_inc(sig, 2)
                act.sem_inc(cm_out, 32)
                for out, n in [(o, 16) for o in f_out] + [(o, 32) for o in ca_out]:
                    act.sem_inc(out, n)

                def step(b, k, first):
                    if k == 0:
                        act.wait_ge(xn_ready, b * NT + 4)
                        act.activation(coef[:, :], norm[:, b, :], ACT.Copy).then_inc(coef_ready, 1)
                        act.wait_ge(coef_ready, b + 1)
                    if k < NT:
                        act.wait_ge(x_full[k % 4], b * (4 * NT) + 16 * (k // 4 + 1))
                        act.wait_ge(conved, b * NT + k + 1)
                        act.activation(xn[:, k % 4, :], x_in[:, k % 4, :], ACT.Identity,
                                       scale=coef[:, 0:1], bias=coef[:, 1:2]).then_inc(xn_ready, 1)
                    at = lagged(b, k, 1, first)
                    if at:
                        m, j = at[0] * NT + at[1], at[1]
                        act.wait_ge(pool_step, 5 * m + 5)
                        act.wait_ge(gated, m + 1)
                        act.activation(gate[:, j % 2, :], psumm[:, j % 2, :], ACT.Sigmoid,
                                       scale=t["mlp"][:, 0:1], bias=t["mlp"][:, 1:2]).then_inc(sig, 1)
                    at = lagged(b, k, 3, first)
                    if at:
                        m, j = at[0] * NT + at[1], at[1]
                        act.wait_ge(conved, m + 5)
                        act.wait_ge(f_out[j % 4], at[0] * (4 * NT) + 16 * (j // 4 + 1))
                        act.activation(f[:, j % 4, :], psF[:, :, :].rearrange("p k n -> p (k n)"), ACT.Identity,
                                       bias=t["bias3"][:, 0:1]).then_inc(f_ready, 1)
                    at = lagged(b, k, 4, first)
                    if at:
                        m, j = at[0] * NT + at[1], at[1]
                        act.wait_ge(turned, m + 2)
                        act.wait_ge(ca_out[j % 2], at[0] * (16 * NT) + 32 * (j // 2 + 1))
                        act.activation(ca[:, j % 2, :], psC[:, :], ACT.Copy).then_inc(ca_ready, 1)
                        act.wait_ge(ca_ready, m + 3)
                        for h in range(2):
                            act.dma_start(bass.AP(maps.tensor, at[0] * plane + (PAD + j * RT + h * RT // 2) * 2 * MAPW + MAPW + PAD,
                                                  [[QR * 2 * MAPW, Q], [2 * MAPW, RT // 2], [1, W]]),
                                          ca[h * C:h * C + Q, j % 2, :].rearrange("p (r w) -> p r w", w=W)).then_inc(ca_out[j % 2], 16)
                    at = lagged(b, k, 3, first)
                    if at:
                        act.wait_ge(f_ready, at[0] * NT + at[1] + 2)
                        act.dma_start(part(fs, at[0], at[1]), f[:, at[1] % 4, :]).then_inc(f_out[at[1] % 4], 16)
                    if k % NT == 4 and not first:
                        m = b - 1 if k < NT else b
                        act.wait_ge(cm_turned, m + 2)
                        act.wait_ge(cm_out, m * 32 + 32)
                        act.activation(cm[:, :, :, :], psM[:, :, :, :], ACT.Copy).then_inc(cm_ready, 1)
                        act.wait_ge(cm_ready, m + 2)
                        for h in range(2):
                            act.dma_start(bass.AP(maps.tensor, m * plane + (PAD + h * P) * 2 * MAPW + PAD, [[2 * MAPW, P], [1, W]]),
                                          cm[:, h, :, :].rearrange("p a w -> p (a w)")).then_inc(cm_out, 16)

                steps(act, step, 5)
                for out, n in [(o, NB * (4 * NT) + 16) for o in f_out] + [(o, NB * (16 * NT) + 32) for o in ca_out]:
                    act.wait_ge(out, n)
                act.wait_ge(cm_out, NB * 32 + 32)

            @block.vector
            def _(dve):
                dve.sem_inc(gated, 2)
                dve.sem_inc(maxed, 1)

                def step(b, k, first):
                    if k < NT:
                        n = b * NT + k
                        s = k % 2
                        rows = xn[:, k % 4, :].rearrange("p (r e w) -> p r e w", e=2, w=W)
                        dve.wait_ge(xn_ready, n + 5)
                        dve.wait_ge(sig, n + 1)
                        dve.tensor_tensor(rmax[:, s, :, :], rows[:, :, 0, :], rows[:, :, 1, :], ALU.max).then_inc(pool_step, 1)
                        dve.tensor_tensor(rsum[:, s, :, :], rows[:, :, 0, :], rows[:, :, 1, :], ALU.add).then_inc(pool_step, 1)
                        dve.wait_ge(pool_step, 5 * n + 1)
                        cols = rmax[:, s, :, :].rearrange("p r (w e) -> p (r w) e", e=2)
                        dve.tensor_tensor(pmax[:, s, :], cols[:, :, 0], cols[:, :, 1], ALU.max).then_inc(pool_step, 1)
                        dve.wait_ge(pool_step, 5 * n + 2)
                        cols = rsum[:, s, :, :].rearrange("p r (w e) -> p (r w) e", e=2)
                        dve.tensor_tensor(psumm[:, s, :], cols[:, :, 0], cols[:, :, 1], ALU.add).then_inc(pool_step, 1)
                        dve.wait_ge(pool_step, 5 * n + 4)
                        dve.scalar_tensor_tensor(psumm[:, s, :], psumm[:, s, :], 0.25, pmax[:, s, :], ALU.mult, ALU.add).then_inc(pool_step, 1)
                    at = lagged(b, k, 1, first)
                    if at:
                        m, j = at[0] * NT + at[1], at[1]
                        dve.wait_ge(sig, m + 3)
                        dve.wait_ge(conved, m + 3)
                        for e in range(2):
                            src = xn[:, j % 4, :].rearrange("p (r e w) -> p r e w", e=2, w=W)[:, :, e, :]
                            dst = prod[:, j % 2, :].rearrange("p (r e w) -> p r e w", e=2, w=W)[:, :, e, :]
                            g = gate[:, j % 2, :].rearrange("p (r w) -> p r w", r=RT // 2).unsqueeze(3).to_broadcast([P, RT // 2, W // 2, 2])
                            last = dve.tensor_tensor(dst.rearrange("p r (w f) -> p r w f", f=2), src.rearrange("p r (w f) -> p r w f", f=2), g, ALU.mult)
                        last.then_inc(gated, 1)
                    at = lagged(b, k, 3, first)
                    if at:
                        m, j = at[0] * NT + at[1], at[1]
                        dve.wait_ge(turned, m + 2)
                        if j == 0:
                            dve.wait_ge(cm_turned, at[0] + 1)
                        for h in range(2):
                            last = dve.tensor_reduce(cmT[:, h, :, j * RT:(j + 1) * RT].rearrange("p q r -> p r q"),
                                                     psT[:, h, :, :].rearrange("p r (o q) -> p r q o", q=Q), AX.X, ALU.max)
                        last.then_inc(maxed, 1)

                steps(dve, step, 3)

            @block.tensor
            def _(pe):
                pe.sem_inc(conved, 4)
                pe.sem_inc(turned, 1)
                pe.sem_inc(cm_turned, 1)

                def step(b, k, first):
                    if k < NT:
                        n = b * NT + k
                        pe.wait_ge(gated, n + 3)
                        pe.wait_ge(f_ready, n + 1)
                        for h in range(2):
                            nc.tensor.matmul(psF[:, h, :], t["w_mix"][:, 1, :], xn[:, k % 4, h * 512:(h + 1) * 512], start=True, stop=False)
                            last = nc.tensor.matmul(psF[:, h, :], t["w_mix"][:, 0, :], prod[:, k % 2, h * 512:(h + 1) * 512], start=False, stop=True)
                        last.then_inc(conved, 1)
                    at = lagged(b, k, 1, first)
                    if at:
                        m, j = at[0] * NT + at[1], at[1]
                        pe.wait_ge(f_ready, m + 2)
                        pe.wait_ge(maxed, m + 1)
                        pe.wait_ge(ca_ready, m + 2)
                        for h in range(2):
                            for r in range(RT):
                                nc.tensor.transpose(psT[:, h, r, :], f[:, j % 4, r * W + h * P:r * W + (h + 1) * P], t["ident"][:, :])
                        for h in range(2):
                            last = nc.tensor.matmul(psC[h * C:(h + 1) * C, :], t["chan_mean"][:, :], f[:, j % 4, h * 512:(h + 1) * 512],
                                                    start=True, stop=True, tile_position=(0, h * C))
                        last.then_inc(turned, 1)
                    if k % NT == 1 and not first:
                        m = b - 1 if k < NT else b
                        pe.wait_ge(maxed, m * NT + NT + 1)
                        pe.wait_ge(cm_ready, m + 1)
                        for a in range(2):
                            for h in range(2):
                                last = nc.tensor.transpose(psM[:, a, h, :], cmT[:, h, 2 * a:2 * a + 2, :].rearrange("p q r -> p (q r)"), t["ident"][:, :])
                        last.then_inc(cm_turned, 1)

                steps(pe, step, 2)


def attention_phase(nc, top, NB, x3, io, t, fs, maps, y):
    RA = 8
    AE = RA * W
    NT = QR // RA
    MW = MAPW - 2
    with Phase(nc) as mem:
        sb = lambda n, s: mem.enter_context(nc.sbuf_tensor("at_" + n, s, F32))
        rows = sb("rows", [P, 4, RA, MW])
        x_in, f_in, a = sb("x_in", [P, 4, AE]), sb("f_in", [P, 4, AE]), sb("a", [P, 2, AE])
        w = sb("w", [P, 4, P])
        wa, quarter = sb("wa", [P, 4, C]), sb("quarter", [P, Q])
        ps = mem.enter_context(nc.psum_tensor("at_ps", [P, 2, 4, 512], F32))
        sem = lambda n: phase_sem(nc, mem, ("at_" + n))
        zeroed, small, widened, conved, sig, scaled, done = sem("zeroed"), sem("small"), sem("widened"), sem("conved"), sem("sig"), sem("scaled"), sem("done")
        r_full, xf_full = [sem(f"r_full{i}") for i in range(4)], [sem(f"xf_full{i}") for i in range(4)]
        y_out = [sem(f"y_out{i}") for i in range(4)]
        plane = MAPW * 2 * MAPW
        part = lambda v, b, k: v[b].rearrange("c (q r) w -> (c q) (r w)", q=Q)[:, k * AE:(k + 1) * AE]
        with nc.Block() as block:
            @block.sync
            def _(sp):
                sp.wait_ge(zeroed, 1)
                n = 1
                sp.dma_start(quarter[:, :], io["quarter_att"]).then_inc(small, 16)
                for q in range(Q):
                    for p in range(4):
                        for s in range(2):
                            if 2 * p + s < 7:
                                sp.dma_start(wa[32 * q + s:32 * q + s + 27:2, p, :], io["att_w"][2 * p + s]).then_inc(small, 16)
                                n += 1
                sp.wait_ge(small, 16 * n)
                with sp.Fori(0, NB) as b:
                    for k in range(NT):
                        sp.wait_ge(conved, b * NT + k + 1)
                        for q in range(Q):
                            for s in range(2):
                                sp.dma_start(rows[32 * q + s:32 * q + s + 31:2, k % 4, :, :],
                                             bass.AP(maps.tensor, b * plane + (QR * q + k * RA) * 2 * MAPW + s,
                                                     [[MAPW, 16], [2 * MAPW, RA], [1, MW]])).then_inc(r_full[k % 4], 16)
                        sp.wait_ge(y_out[k % 4], b * (4 * NT) + 16 * (k // 4 + 1))
                        sp.dma_start(x_in[:, k % 4, :], part(x3, b, k)).then_inc(xf_full[k % 4], 16)
                        sp.dma_start(f_in[:, k % 4, :], part(fs, b, k)).then_inc(xf_full[k % 4], 16)

            @block.tensor
            def _(pe):
                pe.wait_ge(widened, 4)
                pe.sem_inc(conved, 4)
                with pe.Fori(0, NB) as b:
                    for k in range(NT):
                        pe.wait_ge(r_full[k % 4], b * (32 * NT) + 128 * (k // 4 + 1))
                        pe.wait_ge(sig, b * NT + k + 1)
                        for h in range(4):
                            for p in range(4):
                                last = nc.tensor.matmul(ps[:, k % 2, h, :].rearrange("p (r w) -> p r w", w=W), w[:, p, :],
                                                        rows[:, k % 4, 2 * h:2 * h + 2, 2 * p:2 * p + W], start=(p == 0), stop=(p == 3))
                        last.then_inc(conved, 1)

            @block.scalar
            def _(act):
                act.sem_inc(sig, 2)
                for out in y_out:
                    act.sem_inc(out, 16)

                def store(b, k):
                    act.wait_ge(done, b * NT + k + 1)
                    act.dma_start(part(y, b, k), x_in[:, k % 4, :]).then_inc(y_out[k % 4], 16)

                def image(b, first):
                    for k in range(NT):
                        if k >= 1:
                            store(b, k - 1)
                        elif not first:
                            store(b - 1, NT - 1)
                        act.wait_ge(conved, b * NT + k + 5)
                        act.wait_ge(scaled, b * NT + k + 1)
                        act.activation(a[:, k % 2, :], ps[:, k % 2, :, :].rearrange("p h n -> p (h n)"), ACT.Sigmoid,
                                       bias=t["bias_att"][:, 0:1]).then_inc(sig, 1)

                image(0, True)
                with act.Fori(1, NB) as b:
                    image(b, False)
                store(NB - 1, NT - 1)
                for out in y_out:
                    act.wait_ge(out, NB * (4 * NT) + 16)

            @block.vector
            def _(dve):
                dve.memset(wa[:, :, :], 0.0).then_inc(zeroed, 1)
                dve.wait_ge(small, 16 * 29)
                for p in range(4):
                    dve.tensor_tensor(w[:, p, :].rearrange("p (o q) -> p o q", q=Q), wa[:, p, :].unsqueeze(2).to_broadcast([P, C, Q]),
                                      quarter[:, :].unsqueeze(1).to_broadcast([P, C, Q]), ALU.mult).then_inc(widened, 1)
                dve.sem_inc(scaled, 2)
                with dve.Fori(0, NB) as b:
                    for k in range(NT):
                        n = b * NT + k
                        dve.wait_ge(sig, n + 3)
                        dve.wait_ge(xf_full[k % 4], b * (8 * NT) + 32 * (k // 4 + 1))
                        dve.tensor_tensor(f_in[:, k % 4, :], a[:, k % 2, :], f_in[:, k % 4, :], ALU.mult).then_inc(scaled, 1)
                        dve.wait_ge(scaled, n + 3)
                        dve.tensor_tensor(x_in[:, k % 4, :], x_in[:, k % 4, :], f_in[:, k % 4, :], ALU.add).then_inc(done, 1)


def program(nc, NB, io, y, upto=9):
    dram = lambda n, s: nc.dram_tensor(n, s, F32, kind="Internal").ap()
    gates = dram("gates", (4, H, W))
    maps = dram("maps", (NB, MAPW, 2, MAPW))
    Y = dram("modes", (NB, 2, C, M1, M2))
    x1 = dram("x1", (NB, C, H, W))
    pb = dram("pb", (NB, C, Q, Q, QR, QR))
    x2_all = dram("x2", (NB * C * HW + 2 * W,))
    x2 = x2_all[W:W + NB * C * HW].rearrange("(b c h w) -> b c h w", c=C, h=H, w=W)
    x3, fs = dram("x3", (NB, C, H, W)), dram("fs", (NB, C, H, W))
    with ExitStack() as top:
        keep = lambda n, s: top.enter_context(nc.sbuf_tensor("keep_" + n, s, F32))
        t = {"w_dir": keep("w_dir", [P, 4, P]), "w_neg": keep("w_neg", [P, 4, P]), "w_mix": keep("w_mix", [P, 2, P]),
             "ident": keep("ident", [P, P]), "group_avg": keep("group_avg", [P, P]),
             "mask_cq": keep("mask_cq", [P, G]), "mask_jc": keep("mask_jc", [P, G]), "chan_mean": keep("chan_mean", [P, C]), "quarter": keep("quarter", [P, Q]),
             "bias1": keep("bias1", [P, 1]), "bias3": keep("bias3", [P, 1]), "bias_att": keep("bias_att", [P, 1]),
             "mlp": keep("mlp", [P, 2])}
        norm = keep("norm", [P, NB, 3])
        mv = keep("mv", [P, NB, 2])
        guard = bass.AP(x2_all.tensor, 0, [[NB * C * HW + W, 2], [1, W]])
        setup_phase(nc, top, io, gates, guard, t)
        with ExitStack() as spectral:
            bn = spectral.enter_context(nc.sbuf_tensor("bn", [P, NB, C, 6], F32))
            with ExitStack() as modes:
                X = modes.enter_context(nc.sbuf_tensor("X", [P, NB, NG * 64], F32))
                spectrum_phase(nc, top, NB, io["x"], io, bn, X)
                stats_from_rows(nc, top, "st0_", NB, bn[:, :, :, :], t["mask_jc"][:, :], norm)
                mixing_phase(nc, top, NB, io, X, norm, Y, maps)
            if upto < 1:
                return
            inverse_phase(nc, top, NB, io["x"], io, Y, x1, bn)
            stats_from_rows(nc, top, "st1_", NB, bn[:, :, :, :], t["mask_cq"][:, :], norm)
        if upto < 2:
            return
        vertical_phase(nc, top, NB, x1, gates, t, norm, pb)
        if upto < 3:
            return
        horizontal_phase(nc, top, NB, x1, pb, gates, t, norm, x2, mv)
        stats_from_quarters(nc, top, "st2_", NB, mv, t, norm)
        if upto < 4:
            return
        with ExitStack() as dyn:
            kern = dyn.enter_context(nc.sbuf_tensor("kern", [96, NB, JC, 3], F32))
            mean3 = dyn.enter_context(nc.sbuf_tensor("mean3", [96, NB, JC], F32))
            kernels_phase(nc, top, NB, mv, norm, io, kern, mean3)
            depthwise_phase(nc, top, NB, x2, kern, mean3, io, norm, x3, mv)
        stats_from_quarters(nc, top, "st3_", NB, mv, t, norm)
        if upto < 5:
            return
        gate_phase(nc, top, NB, x3, io, t, norm, fs, maps)
        if upto < 6:
            return
        attention_phase(nc, top, NB, x3, io, t, fs, maps, y)


def constants():
    k, n = np.arange(M1), np.arange(H)
    ang = 2 * np.pi * ((n[:, None] * k[None, :]) % H) / H
    cos, sin = np.cos(ang), np.sin(ang)
    weight = np.where(k == 0, 1.0, 2.0) / HW
    inv_w = np.concatenate([weight[:, None] * cos.T, -weight[:, None] * sin.T])
    p = np.arange(P)
    c_of, q_of = p // Q, p % Q
    r96 = np.arange(96)
    dy, c8, q3 = r96 // 32, (r96 % 32) // Q, r96 % Q
    sel = np.zeros((P, JC, 96))
    for j in range(JC):
        sel[:, j] = (c_of[:, None] == CJ * j + c8[None, :]) & (q_of[:, None] == q3[None, :])
    centre = np.zeros((96, JC, 3))
    centre[dy == 1, :, 1] = 1.0
    inside = np.ones((96, 2))
    inside[(dy == 0) & (q3 == 0), 0] = 0.0
    inside[(dy == 2) & (q3 == Q - 1), 1] = 0.0
    out = {
        "dft_h": np.concatenate([cos, sin], 1),
        "dft_w": np.stack([np.concatenate([cos, -sin], 1), np.concatenate([-sin, -cos], 1)], 1),
        "idft_h": np.concatenate([cos.T, sin.T]),
        "idft_w": np.kron(np.eye(2), inv_w),
        "ident": np.eye(P),
        "group_avg": (c_of[:, None] // 2 == c_of[None, :] // 2) / (2.0 * Q),
        "mask_cq": (c_of[:, None] // 2 == np.arange(G)[None, :]),
        "mask_jc": ((p % C)[:, None] // 2 == np.arange(G)[None, :]),
        "chan_mean": (q_of[:, None] == np.arange(C)[None, :]) / float(C),
        "quarter": q_of[:, None] == np.arange(Q)[None, :],
        "quarter_att": (p // C)[:, None] == np.arange(Q)[None, :],
        "select_96": sel.reshape(P, JC * 96),
        "centre_96": centre.reshape(96, 12),
        "inside_96": inside,
        "eye_96": np.concatenate([np.eye(32)] * 3),
    }
    return {n: np.ascontiguousarray(v, np.float32) for n, v in out.items()}


def layouts(x, L0_conv_coeff_real, L0_conv_coeff_imag, L0_conv_proj, L1_conv_weights, L1_conv_conv_w, L1_conv_conv_b,
            L2_conv_w1, L2_conv_b1, L2_conv_w2, L2_conv_b2, L3_conv_mlp_w, L3_conv_mlp_b, L3_conv_conv_w, L3_conv_conv_b,
            L3_conv_convout_w, L3_conv_convout_b):
    a = np.asarray
    up, down, left, right = a(L1_conv_weights)
    modes_last = lambda v: a(v).reshape(C, C, NG, J, M2).transpose(0, 2, 4, 3, 1)
    out = {
        "x": a(x), "coeff_real": modes_last(L0_conv_coeff_real), "coeff_imag": modes_last(L0_conv_coeff_imag), "proj_T": a(L0_conv_proj).T,
        "scan_w": np.stack([left, right, up.T, down.T]),
        "conv1_T": a(L1_conv_conv_w).T, "conv1_b": a(L1_conv_conv_b),
        "mlp_w1": a(L2_conv_w1), "mlp_b1": a(L2_conv_b1).reshape(P, 1), "mlp_w2": a(L2_conv_w2), "mlp_b2": a(L2_conv_b2).reshape(1, -1),
        "mlp_w": a(L3_conv_mlp_w).reshape(1), "mlp_b": a(L3_conv_mlp_b).reshape(1),
        "conv3_T": a(L3_conv_conv_w).reshape(C, 2 * C).T, "conv3_b": a(L3_conv_conv_b),
        "att_w": a(L3_conv_convout_w).transpose(3, 2, 1, 0).reshape(7, 14, C), "att_b": a(L3_conv_convout_b),
    }
    return {n: np.ascontiguousarray(v) for n, v in out.items()}


def kernel(**inputs):
    import concourse.bacc as bacc
    from concourse.bass_utils import run_bass_kernel_spmd

    nc = bacc.Bacc("TRN2", target_bir_lowering=False, num_devices=1)
    arrays = {**layouts(**inputs), **constants()}
    io = {n: nc.dram_tensor(n, v.shape, mybir.dt.from_np(v.dtype), kind="ExternalInput").ap() for n, v in arrays.items()}
    NB = arrays["x"].shape[0]
    y = nc.dram_tensor("y", (NB, C, H, W), F32, kind="ExternalOutput").ap()
    program(nc, NB, io, y)
    r = run_bass_kernel_spmd(nc, [arrays], core_ids=[0])
    return r.results[0]["y"]
```
